# Optimizing a Trainium2 kernel written in Bass

```python
import numpy as np
import jax
import jax.numpy as jnp

def _softmax(x, axis=-1):
    return jax.nn.softmax(x, axis=axis)
def _gelu(x):
    return jax.nn.gelu(x, approximate=True)
def _silu(x):
    return jax.nn.silu(x)
def _sigmoid(x):
    return jax.nn.sigmoid(x)
def _layernorm(x, axis=-1, eps=1e-5):
    m = jnp.mean(x, axis=axis, keepdims=True)
    v = jnp.var(x, axis=axis, keepdims=True)
    return (x - m) / jnp.sqrt(v + eps)
def _scatter_add(tgt, idx, src, axis=0):
    return tgt.at[idx].add(src)
def _segment_sum(src, seg, n):
    return jax.ops.segment_sum(src, seg, n)

kernel_name = 'mk_conv_preact_d2_conv_nchw256_c097e9'

def setup_inputs(seed: int = 0):
    np.random.seed(seed)
    _w = jnp.asarray
    def _rec_inputs():
        import jax
        import jax.numpy as jnp
        _gk = jax.random.key(seed)
        x = -0.0002928 + 1 * jax.random.normal(jax.random.fold_in(_gk, 1), (4, 256, 64, 64), jnp.float32)
        return x
    x = _rec_inputs()
    def _L0_conv_setup():
        import jax, jax.numpy as jnp
        import numpy as np
        C = 256
        EPS = 1e-05
        key = jax.random.key(seed)
        ks = jax.random.split(key, 10)
        N, H, W = (4, 64, 64)
        Ch = C // 2
        sc = 1.0 / np.sqrt(C)
        sch = 1.0 / np.sqrt(Ch)
        return {'x': jax.random.normal(ks[0], (N, C, H, W), dtype=jnp.float32), 'cfc': jax.random.normal(ks[1], (C, 2), dtype=jnp.float32) * 0.1, 'theta_w': jax.random.normal(ks[2], (Ch, C), dtype=jnp.float32) * sc, 'theta_b': jax.random.normal(ks[3], (Ch,), dtype=jnp.float32) * 0.01, 'phi_w': jax.random.normal(ks[4], (Ch, C), dtype=jnp.float32) * sc, 'phi_b': jax.random.normal(ks[5], (Ch,), dtype=jnp.float32) * 0.01, 'g_w': jax.random.normal(ks[6], (Ch, C), dtype=jnp.float32) * sc, 'g_b': jax.random.normal(ks[7], (Ch,), dtype=jnp.float32) * 0.01, 'out_w': jax.random.normal(ks[8], (C, Ch), dtype=jnp.float32) * sch, 'out_b': jax.random.normal(ks[9], (C,), dtype=jnp.float32) * 0.01}
    _L0_conv_all = _L0_conv_setup()
    _L0_conv_in = {k: v for k, v in _L0_conv_all.items() if k in ('cfc', 'theta_w', 'theta_b', 'phi_w', 'phi_b', 'g_w', 'g_b', 'out_w', 'out_b', )}
    del _L0_conv_all

    def _L1_conv_setup():
        import jax, jax.numpy as jnp
        import numpy as np
        HEADS = 8
        HID = 256
        EPS = 1e-05
        key = jax.random.key(seed)
        k1, k2, k3, k4 = jax.random.split(key, 4)
        B, C, H, W = (16, 256, 64, 64)
        x = jax.random.normal(k1, (B, C, H, W), dtype=jnp.float32)
        w_qkv = jax.random.normal(k2, (3 * HID, C), dtype=jnp.float32) * (1.0 / np.sqrt(C))
        w_out = jax.random.normal(k3, (C, HID), dtype=jnp.float32) * (1.0 / np.sqrt(HID))
        b_out = jax.random.normal(k4, (C,), dtype=jnp.float32) * 0.01
        g = jnp.ones((C,), dtype=jnp.float32)
        return {'x': x, 'w_qkv': w_qkv, 'w_out': w_out, 'b_out': b_out, 'g': g}
    _L1_conv_all = _L1_conv_setup()
    _L1_conv_in = {k: v for k, v in _L1_conv_all.items() if k in ('w_qkv', 'w_out', 'b_out', 'g', )}
    del _L1_conv_all

    return {
        "x": x,
        "L0_conv_cfc": _L0_conv_in["cfc"],
        "L0_conv_theta_w": _L0_conv_in["theta_w"],
        "L0_conv_theta_b": _L0_conv_in["theta_b"],
        "L0_conv_phi_w": _L0_conv_in["phi_w"],
        "L0_conv_phi_b": _L0_conv_in["phi_b"],
        "L0_conv_g_w": _L0_conv_in["g_w"],
        "L0_conv_g_b": _L0_conv_in["g_b"],
        "L0_conv_out_w": _L0_conv_in["out_w"],
        "L0_conv_out_b": _L0_conv_in["out_b"],
        "L1_conv_w_qkv": _L1_conv_in["w_qkv"],
        "L1_conv_w_out": _L1_conv_in["w_out"],
        "L1_conv_b_out": _L1_conv_in["b_out"],
        "L1_conv_g": _L1_conv_in["g"],
    }

def reference(x, L0_conv_cfc, L0_conv_theta_w, L0_conv_theta_b, L0_conv_phi_w, L0_conv_phi_b, L0_conv_g_w, L0_conv_g_b, L0_conv_out_w, L0_conv_out_b, L1_conv_w_qkv, L1_conv_w_out, L1_conv_b_out, L1_conv_g):
    import jax
    import jax.numpy as jnp
    def _L0_conv_ref(x, cfc, theta_w, theta_b, phi_w, phi_b, g_w, g_b, out_w, out_b):
        import jax, jax.numpy as jnp
        import numpy as np
        C = 256
        EPS = 1e-05
        N, Cc, H, W = x.shape
        L = H * W
        xf = x.reshape(N, Cc, L)
        mean = jnp.mean(xf, axis=2)
        var = jnp.var(xf, axis=2, ddof=1) + EPS
        std = jnp.sqrt(var)
        z = mean * cfc[None, :, 0] + std * cfc[None, :, 1]
        gate = jax.nn.sigmoid(z)[:, :, None]
        s = xf * gate
        theta = jnp.einsum('oc,ncl->nol', theta_w, s) + theta_b[None, :, None]
        phi = jnp.einsum('oc,ncl->nol', phi_w, s) + phi_b[None, :, None]
        g = jnp.einsum('oc,ncl->nol', g_w, s) + g_b[None, :, None]
        attn = jax.nn.softmax(jnp.einsum('nci,ncj->nij', theta, phi), axis=-1)
        nl = jnp.einsum('ncj,nij->nci', g, attn)
        nl = jnp.einsum('oc,ncl->nol', out_w, nl) + out_b[None, :, None]
        out = s + nl
        return out.reshape(N, Cc, H, W)

    def _L1_conv_ref(x, w_qkv, w_out, b_out, g):
        import jax, jax.numpy as jnp
        import numpy as np
        HEADS = 8
        HID = 256
        EPS = 1e-05
        B, C, H, W = x.shape
        n = H * W
        dh = HID // HEADS
        scale = dh ** (-0.5)
        qkv = jnp.einsum('bchw,oc->bohw', x, w_qkv)
        qkv = qkv.reshape(B, 3, HEADS, dh, n)
        q, k, v = (qkv[:, 0], qkv[:, 1], qkv[:, 2])
        q = jax.nn.softmax(q, axis=2) * scale
        k = jax.nn.softmax(k, axis=3)
        v = v / n
        context = jnp.einsum('bhdn,bhen->bhde', k, v)
        out = jnp.einsum('bhde,bhdn->bhen', context, q)
        out = out.reshape(B, HID, H, W)
        y = jnp.einsum('bchw,oc->bohw', out, w_out) + b_out[None, :, None, None]
        mean = jnp.mean(y, axis=1, keepdims=True)
        var = jnp.var(y, axis=1, keepdims=True)
        return (y - mean) * jax.lax.rsqrt(var + EPS) * g[None, :, None, None]

    def _gn(v, G=32, eps=1e-5):
        B_, C_, H_, W_ = v.shape
        g = v.reshape(B_, G, C_ // G, H_, W_)
        m = jnp.mean(g, axis=(2, 3, 4), keepdims=True)
        s = jnp.var(g, axis=(2, 3, 4), keepdims=True)
        return ((g - m) / jnp.sqrt(s + eps)).reshape(v.shape)

    def _ln_c(v, eps=1e-6):
        m = jnp.mean(v, axis=1, keepdims=True)
        s = jnp.var(v, axis=1, keepdims=True)
        return (v - m) / jnp.sqrt(s + eps)

    def _ln_t(v, eps=1e-5):
        m = jnp.mean(v, axis=-1, keepdims=True)
        s = jnp.var(v, axis=-1, keepdims=True)
        return (v - m) / jnp.sqrt(s + eps)

    def _to_tokens(v):
        B_, C_, H_, W_ = v.shape
        return v.reshape(B_, C_, H_ * W_).transpose(0, 2, 1)
    def _from_tokens(t, like):
        B_, C_, H_, W_ = like.shape
        return t.transpose(0, 2, 1).reshape(B_, C_, H_, W_)

    x = x + _L0_conv_ref(_gn(x), L0_conv_cfc, L0_conv_theta_w, L0_conv_theta_b, L0_conv_phi_w, L0_conv_phi_b, L0_conv_g_w, L0_conv_g_b, L0_conv_out_w, L0_conv_out_b)
    x = x + _L1_conv_ref(_gn(x), L1_conv_w_qkv, L1_conv_w_out, L1_conv_b_out, L1_conv_g)
    return x


_drawn_inputs = setup_inputs


def setup_inputs(seed=0):
    import zlib

    import numpy as np

    out = dict(_drawn_inputs(seed))
    spreads = {'L1_conv_g': (1.0, 0.2)}
    factors = {'L0_conv_cfc': 3.0,
     'L0_conv_theta_b': 8.0,
     'L0_conv_phi_b': 8.0,
     'L0_conv_g_b': 8.0,
     'L0_conv_out_b': 8.0,
     'L1_conv_w_qkv': 8.0,
     'L1_conv_w_out': 8.0}
    for name, (base, spread) in spreads.items():
        noise = np.random.default_rng([zlib.crc32(name.encode()), seed]).standard_normal(out[name].shape)
        drawn = base * np.exp(spread * noise) if base else spread * noise
        out[name] = jnp.asarray(drawn.astype(out[name].dtype))
    for name, factor in factors.items():
        out[name] = (out[name] * factor).astype(out[name].dtype)
    return out
```

```python
from contextlib import ExitStack

import concourse.bass as bass
from concourse import mybir

ALU = mybir.AluOpType
ACT = mybir.ActivationFunctionType
F32 = mybir.dt.float32
F32R = mybir.dt.float32r
AX = mybir.AxisListType

P = 128
N, C, L = 4, 256, 4096
KT = C // P
CH = C // 2
CK = 512
NCK = L // CK
QT = CK // P
NQ = 4
QW = L // NQ
JQ = QW // P
JT = L // P
GROUPS = 32
GC = C // GROUPS
EPS_GN = 1e-5
EPS_STD = 1e-5
EPS_LN = 1e-5
HEADS, DH = 8, 32

C_CFC0, C_CFC1, C_THB, C_PHB, C_GB, C_OUTB, C_BOUT, C_LNG = 0, 2, 4, 5, 6, 7, 9, 11
N_PAR = 13


def nonlocal_block(nc, x, par, wth, wph, wg, wout, x1):
    ctx = ExitStack()
    with ctx:
        def sb(name, shape, dt=F32):
            return ctx.enter_context(nc.sbuf_tensor(name, shape, dt))

        def sem(name):
            return ctx.enter_context(nc.semaphore(name))

        probs = sb("probs", [P, QT * NQ, QW])
        phi_h = sb("phi_h", [P, L], F32R)
        phi_l = sb("phi_l", [P, L], F32R)
        gT_h = sb("gT_h", [P, JT, P], F32R)
        gT_l = sb("gT_l", [P, JT, P], F32R)
        xs = sb("xs", [P, KT, L])
        pT_h = sb("pT_h", [P, 4, CK], F32R)
        pT_l = sb("pT_l", [P, 4, CK], F32R)
        th_h = sb("th_h", [P, CK], F32R)
        th_l = sb("th_l", [P, CK], F32R)
        sq = sb("sq", [P, KT, CK])
        res = sb("res", [P, KT, CK])
        o_n = sb("o_n", [P, CK])
        rb = sb("rb", [P, CK])
        dg = sb("dg", [P, QT, P])
        wth_s = sb("wth_s", [P, KT, CH])
        wph_s = sb("wph_s", [P, KT, CH])
        wg_s = sb("wg_s", [P, KT, CH])
        wout_s = sb("wout_s", [P, C])
        pr = sb("pr", [P, N_PAR])
        ident = sb("ident", [P, P])
        ones = sb("ones", [P, P])
        grp = sb("grp", [P, P])
        tick = sb("tick", [P, 3])
        bst = sb("bst", [P, KT, NCK, 6])
        mv = sb("mv", [P, KT, 2])
        me = sb("me", [P, 2, KT])
        gs = sb("gs", [P, 2, KT])
        sm = sb("sm", [P, 12, KT])
        ab = sb("ab", [P, 3, KT])
        mx = sb("mx", [P, QT, NQ])
        nm = sb("nm", [P, QT])
        den = sb("den", [P, 2, QT, NQ])
        dsum = sb("dsum", [P, 2, QT])

        psA = ctx.enter_context(nc.psum_tensor("psA", [P, 2, 2 * CK], F32))
        psT = ctx.enter_context(nc.psum_tensor("psT", [P, 3, CK], F32))
        psO = ctx.enter_context(nc.psum_tensor("psO", [P, CK], F32))

        w_loaded = sem("w_loaded")
        x_loaded = sem("x_loaded")
        sq_loaded = sem("sq_loaded")
        res_loaded = sem("res_loaded")
        res_free = sem("res_free")
        consts = sem("consts")
        const_step = sem("const_step")
        gp_done = sem("gp_done")
        stats = sem("stats")
        step = sem("step")
        root = sem("root")
        ab_ready = sem("ab_ready")
        s0_ready = sem("s0_ready")
        s1_ready = sem("s1_ready")
        sq_ready = sem("sq_ready")
        res_ready = sem("res_ready")
        phi_mm = sem("phi_mm")
        g_mm = sem("g_mm")
        g_copied = sem("g_copied")
        phih_ready = sem("phih_ready")
        g_turned = sem("g_turned")
        gTh_ready = sem("gTh_ready")
        gTl_ready = sem("gTl_ready")
        scored = sem("scored")
        a_used = sem("a_used")
        negmax = sem("negmax")
        exped = sem("exped")
        t_ready = sem("t_ready")
        t_used = sem("t_used")
        pTh_ready = sem("pTh_ready")
        thh_ready = sem("thh_ready")
        sums = sem("sums")
        dg_ready = sem("dg_ready")
        rb_ready = sem("rb_ready")
        pv_done = sem("pv_done")

        A_IMG = NCK + NCK * QT * NQ

        def a_idx(n, b, t, c):
            return n * A_IMG + NCK + b * (QT * NQ) + t * NQ + c

        T_STAGE = JT + 1 + KT + 1
        T_IMG = 2 + NCK * T_STAGE - 2
        T_INV, T_OUT, T_TH = JT, JT + 1, JT + 1 + KT
        assert T_STAGE % 3 == 0 and T_IMG % 3 == 0

        def t_base(n, b):
            late = 1 if isinstance(b, int) and b == NCK - 1 else 0
            return n * T_IMG + 2 + b * T_STAGE - late

        def t_slot(e, k):
            return (2 + k - e) % 3

        def cell(par, t, q):
            return probs[:, (t * NQ + q) if par == 0 else (q * NQ + t), :]

        x_v = x.rearrange("n (k p) l -> n p k l", p=P)
        x1_v = x1.rearrange("n (k p) l -> n p k l", p=P)
        block = ctx.enter_context(nc.Block())

        @block.sync
        def _(sp):
            for dst, src in ((wth_s[:], wth.rearrange("(k p) o -> p k o", p=P)),
                             (wph_s[:], wph.rearrange("(k p) o -> p k o", p=P)),
                             (wg_s[:], wg.rearrange("(k p) o -> p k o", p=P)),
                             (wout_s[:], wout[:, :]), (pr[:], par[:, :])):
                sp.dma_start(dst, src).then_inc(w_loaded, 16)

            def stage(n, b, has_th):
                sp.wait_ge(res_free, 16 * (n * NCK + b + 1))
                sp.dma_start(res[:], x_v[n, :, :, bass.ds(b * CK, CK)]).then_inc(res_loaded, 16)
                if has_th:
                    sp.wait_ge(t_ready, n * T_IMG + b * T_STAGE + 2)
                    sp.dma_start(sq[:], x_v[n, :, :, bass.ds((b + 2) * CK, CK)]).then_inc(sq_loaded, 16)
                sp.wait_ge(t_used, t_base(n, b) + T_TH)
                sp.dma_start(x1_v[n, :, :, bass.ds(b * CK, CK)], res[:]).then_inc(res_free, 16)

            def load_x(n):
                for k in range(KT):
                    sp.dma_start(xs[:, k, :], x_v[n, :, k, :]).then_inc(x_loaded, 16)

            def image(n, last):
                sp.dma_start(sq[:], x_v[n, :, :, 0:CK]).then_inc(sq_loaded, 16)
                sp.wait_ge(t_ready, n * T_IMG + 1)
                sp.dma_start(sq[:], x_v[n, :, :, CK:2 * CK]).then_inc(sq_loaded, 16)
                sp.wait_ge(phi_mm, (n + 1) * NCK)
                if last:
                    sp.sem_inc(x_loaded, 16 * KT)
                else:
                    load_x(n + 1)
                with sp.Fori(0, (NCK - 2) // 2) as pair:
                    for e in range(2):
                        stage(n, pair * 2 + e, True)
                stage(n, NCK - 2, False)
                stage(n, NCK - 1, False)

            load_x(0)
            with sp.Fori(0, N - 1) as n:
                image(n, False)
            image(N - 1, True)
            sp.wait_ge(res_free, 16 * (N * NCK + 1))

        @block.gpsimd
        def _(pool):
            pool.memset(ident[:], 0.0).then_inc(const_step, 1)
            pool.memset(ones[:], 1.0).then_inc(consts, 1)
            pool.memset(tick[:], 0.0).then_inc(res_free, 16)
            pool.memset(grp[:], 1.0 / GC).then_inc(const_step, 1)
            pool.wait_ge(const_step, 2)
            pool.affine_select(out=ident[:], in_=ident[:], compare_op=ALU.not_equal, fill=1.0, base=0,
                               pattern=[[-1, P]], channel_multiplier=1).then_inc(consts, 1)
            gv = grp[:].rearrange("p (a c) -> p a c", c=GC)
            pool.affine_select(out=gv, in_=gv, compare_op=ALU.is_ge, fill=0.0, base=0,
                               pattern=[[-GC, P // GC], [0, GC]], channel_multiplier=1).then_inc(const_step, 1)
            pool.wait_ge(const_step, 3)
            pool.affine_select(out=gv, in_=gv, compare_op=ALU.is_ge, fill=0.0, base=GC - 1,
                               pattern=[[GC, P // GC], [0, GC]], channel_multiplier=-1).then_inc(consts, 1)

            def carry(i):
                pool.tensor_tensor(tick[:, i:i + 1], ab[:, 0, 0:1], ab[:, 0, 0:1], ALU.add)

            def s_block(n, b):
                pool.wait_ge(sq_loaded, 16 * (n * NCK + b + 1))
                carry(0)
                for k in range(KT):
                    ins = pool.tensor_scalar(sq[:, k, :], sq[:, k, :], ab[:, 0, k:k + 1], ab[:, 1, k:k + 1],
                                             ALU.mult, ALU.add)
                ins.then_inc(sq_ready, 1)

            def stage(n, b, has_th):
                pool.wait_ge(res_loaded, 16 * (n * NCK + b + 1))
                carry(2)
                for k in range(KT):
                    ins = pool.tensor_scalar(res[:, k, :], res[:, k, :], ab[:, 2, k:k + 1], ab[:, 1, k:k + 1],
                                             ALU.mult, ALU.add)
                ins.then_inc(res_ready, 1)
                if has_th:
                    s_block(n, b + 2)

            with pool.Fori(0, N) as n:
                pool.wait_ge(ab_ready, n + 1)
                s_block(n, 0)
                s_block(n, 1)
                with pool.Fori(0, (NCK - 2) // 2) as pair:
                    for e in range(2):
                        stage(n, pair * 2 + e, True)
                stage(n, NCK - 2, False)
                stage(n, NCK - 1, False)

        @block.tensor
        def _(pe):
            pe.wait_ge(consts, 3)
            pe.wait_ge(w_loaded, 80)

            def three_pass(out, lh, ll, rh, rl, start, stop):
                pe.matmul(out, lh, rh, start=start, stop=False)
                pe.matmul(out, ll, rh, start=False, stop=False)
                return pe.matmul(out, lh, rl, start=False, stop=stop)

            def theta(n, b, idx, slot):
                pe.wait_ge(sq_ready, n * NCK + b + 1)
                if idx is not None:
                    pe.wait_ge(t_used, idx - 2)
                for k in range(KT):
                    ins = pe.matmul(psT[:, slot, :], wth_s[:, k, :], sq[:, k, :], start=(k == 0), stop=(k == KT - 1))
                ins.then_inc(t_ready, 1)

            def scores(n, b, t, c):
                pe.wait_ge(a_used, a_idx(n, b, t, c) - 1)
                for h in range(2):
                    cols = slice(c * QW + h * CK, c * QW + (h + 1) * CK)
                    q = slice(t * P, (t + 1) * P)
                    ins = three_pass(psA[:, c % 2, h * CK:(h + 1) * CK], th_h[:, q], th_l[:, q],
                                     phi_h[:, cols], phi_l[:, cols], True, True)
                ins.then_inc(scored, 1)

            def turn(n, b, e, par, j):
                base = t_base(n, b)
                if j % JQ == 0:
                    pe.wait_ge(exped, (n * NCK + b + 1) * QT * NQ - NQ + j // JQ + 1)
                pe.wait_ge(t_used, base + max(j - 2, -1))
                for t in range(QT):
                    ins = pe.transpose(psT[:, t_slot(e, j), t * P:(t + 1) * P],
                                       cell(par, t, j // JQ)[:, (j % JQ) * P:(j % JQ + 1) * P], ident[:])
                ins.then_inc(t_ready, 1)

            def weigh(n, b, j):
                pe.wait_ge(t_used, t_base(n, b) + j + 1)
                s = j % 4
                ins = three_pass(psO[:, :], gT_h[:, j, :], gT_l[:, j, :], pT_h[:, s, :], pT_l[:, s, :],
                                 j == 0, j == JT - 1)
                if j == JT - 1:
                    ins.then_inc(pv_done, 1)

            def group_means(n):
                pe.wait_ge(step, n * STEPS + 3)
                pe.matmul(psA[:, 0, 0:2 * KT], grp[:], me[:].rearrange("p a k -> p (a k)"),
                          start=True, stop=True).then_inc(gp_done, 1)

            def stage(n, b, e, par, has_a, has_th):
                base = t_base(n, b)
                for j in range(JQ):
                    turn(n, b, e, par, j)
                    if j >= 2:
                        weigh(n, b, j - 2)
                for t in range(QT - 1):
                    for c in range(NQ):
                        if has_a:
                            scores(n, b + 1, t, c)
                        elif (t, c) == (1, 0):
                            group_means(n + 1)
                        for j in range(JQ * (t + 1) + 2 * c, JQ * (t + 1) + 2 * c + 2):
                            turn(n, b, e, par, j)
                            weigh(n, b, j - 2)
                pe.wait_ge(dg_ready, n * NCK + b + 1)
                pe.wait_ge(t_used, base + T_INV - 2)
                pe.matmul(psT[:, t_slot(e, T_INV), :], ones[:], dg[:].rearrange("p t q -> p (t q)"),
                          start=True, stop=True).then_inc(t_ready, 1)
                if has_a:
                    scores(n, b + 1, QT - 1, 0)
                weigh(n, b, JT - 2)
                weigh(n, b, JT - 1)
                if has_a:
                    for c in range(1, NQ):
                        scores(n, b + 1, QT - 1, c)
                pe.wait_ge(t_used, base + T_INV + 1)
                for k in range(KT):
                    pe.matmul(psT[:, t_slot(e, T_OUT + k), :], wout_s[:, k * P:(k + 1) * P], o_n[:],
                              start=True, stop=True).then_inc(t_ready, 1)
                if has_th:
                    theta(n, b + 2, base + T_TH, t_slot(e, T_TH))

            group_means(0)
            with pe.Fori(0, N) as n:
                for c in range(NCK + 1):
                    if c == 2:
                        theta(n, 0, None, 0)
                    if c < NCK:
                        pe.wait_ge(s0_ready, n * NCK + c + 1)
                        pe.wait_ge(s1_ready, n * NCK + c + 1)
                        if c >= 2:
                            pe.wait_ge(a_used, n * A_IMG + c - 1)
                        for w, half, done in ((wg_s, 1, g_mm), (wph_s, 0, phi_mm)):
                            for k in range(KT):
                                ins = pe.matmul(psA[:, c % 2, half * CK:(half + 1) * CK], w[:, k, :],
                                                xs[:, k, c * CK:(c + 1) * CK], start=(k == 0), stop=(k == KT - 1))
                            ins.then_inc(done, 1)
                    if c >= 1:
                        pe.wait_ge(g_copied, n * NCK + c)
                        if c >= 2:
                            pe.wait_ge(gTl_ready, n * NCK + c - 1)
                        for t in range(QT):
                            ins = pe.transpose(psO[:, t * P:(t + 1) * P],
                                               probs[:, (c - 1) % 2, t * P:(t + 1) * P], ident[:])
                        ins.then_inc(g_turned, 1)
                pe.wait_ge(a_used, n * A_IMG + NCK)
                pe.wait_ge(t_used, n * T_IMG + 1)
                for t in range(QT):
                    for c in range(NQ):
                        scores(n, 0, t, c)
                pe.wait_ge(gTl_ready, (n + 1) * NCK)
                theta(n, 1, None, 1)
                with pe.Fori(0, (NCK - 2) // 2) as pair:
                    for e in range(2):
                        stage(n, pair * 2 + e, 0, e, True, True)
                stage(n, NCK - 2, 0, 0, True, False)
                stage(n, NCK - 1, 1, 1, False, False)

        @block.scalar
        def _(act):
            def exp(n, b, par, t, c):
                if c == 0:
                    act.wait_ge(negmax, (n * NCK + b) * QT + t + 1)
                act.activation(cell(par, t, c), cell(par, t, c), ACT.Exp, bias=nm[:, t:t + 1],
                               accum_out=den[:, par, t, c:c + 1]).then_inc(exped, 1)

            def gate_root(n, i):
                src, dst, func, scale, at = ((3, 4, ACT.Sqrt, 1.0, R1), (7, 8, ACT.Sqrt, 1.0, R2),
                                             (9, 10, ACT.Exp, -1.0, R3))[i]
                act.wait_ge(step, n * STEPS + at)
                act.activation(sm[:, dst, :], sm[:, src, :], func, scale=scale).then_inc(root, 1)

            def theta_h(n, idx, slot):
                act.wait_ge(t_ready, idx + 1)
                act.activation(th_h[:], psT[:, slot, :], ACT.Identity,
                               bias=pr[:, C_THB:C_THB + 1]).then_inc(thh_ready, 1)

            def prob_h(n, b, e, j):
                act.wait_ge(t_ready, t_base(n, b) + j + 1)
                act.activation(pT_h[:, j % 4, :], psT[:, t_slot(e, j), :], ACT.Copy).then_inc(pTh_ready, 1)

            def stage(n, b, e, par, has_a, has_th):
                for j in range(JQ):
                    prob_h(n, b, e, j)
                    if j % 2 == 1 and j < 7:
                        exp(n, b, par, QT - 1, (j + 1) // 2)
                for t in range(QT - 1):
                    for c in range(NQ):
                        if has_a and t >= 1:
                            exp(n, b + 1, 1 - par, t - 1, c)
                        for j in range(JQ * (t + 1) + 2 * c, JQ * (t + 1) + 2 * c + 2):
                            prob_h(n, b, e, j)
                        if not has_a and t == 1 and c >= 1:
                            gate_root(n + 1, c - 1)
                act.wait_ge(t_ready, t_base(n, b) + T_INV + 1)
                act.activation(rb[:], psT[:, t_slot(e, T_INV), :], ACT.Copy).then_inc(rb_ready, 1)
                if has_a:
                    for c in range(NQ):
                        exp(n, b + 1, 1 - par, QT - 2, c)
                    exp(n, b + 1, 1 - par, QT - 1, 0)
                if has_th:
                    theta_h(n, t_base(n, b) + T_TH, t_slot(e, T_TH))

            act.wait_ge(w_loaded, 80)
            for i in range(3):
                gate_root(0, i)
            with act.Fori(0, N) as n:
                act.wait_ge(ab_ready, n + 1)
                for c in range(2):
                    act.activation(xs[:, 0, c * CK:(c + 1) * CK], xs[:, 0, c * CK:(c + 1) * CK], ACT.Identity,
                                   bias=ab[:, 1, 0:1], scale=ab[:, 0, 0:1]).then_inc(s0_ready, 1)
                for c in range(NCK + 1):
                    if c == 2:
                        theta_h(n, n * T_IMG, 0)
                    if c + 2 < NCK:
                        cols = slice((c + 2) * CK, (c + 3) * CK)
                        act.activation(xs[:, 0, cols], xs[:, 0, cols], ACT.Identity,
                                       bias=ab[:, 1, 0:1], scale=ab[:, 0, 0:1]).then_inc(s0_ready, 1)
                    if c < NCK:
                        act.wait_ge(g_mm, n * NCK + c + 1)
                        act.activation(probs[:, c % 2, 0:CK], psA[:, c % 2, CK:2 * CK], ACT.Identity,
                                       bias=pr[:, C_GB:C_GB + 1]).then_inc(g_copied, 1)
                        act.wait_ge(phi_mm, n * NCK + c + 1)
                        act.activation(phi_h[:, c * CK:(c + 1) * CK], psA[:, c % 2, 0:CK], ACT.Identity,
                                       bias=pr[:, C_PHB:C_PHB + 1]).then_inc(phih_ready, 1)
                    if c >= 1:
                        act.wait_ge(g_turned, n * NCK + c)
                        act.activation(gT_h[:, (c - 1) * QT:c * QT, :],
                                       psO[:].rearrange("p (t q) -> p t q", t=QT), ACT.Copy).then_inc(gTh_ready, 1)
                for t in range(QT - 1):
                    for c in range(NQ):
                        exp(n, 0, 0, t, c)
                exp(n, 0, 0, QT - 1, 0)
                theta_h(n, n * T_IMG + 1, 1)
                with act.Fori(0, (NCK - 2) // 2) as pair:
                    for e in range(2):
                        stage(n, pair * 2 + e, 0, e, True, True)
                stage(n, NCK - 2, 0, 0, True, False)
                stage(n, NCK - 1, 1, 1, False, False)

        @block.vector
        def _(dve):
            tt, ts_ = dve.tensor_tensor, dve.tensor_scalar
            mean, var = mv[:, :, 0], mv[:, :, 1]

            def chunk_stats(c):
                for k in range(KT):
                    ins = dve.bn_stats(bst[:, k, bass.ds(c, 1), :].rearrange("p a s -> p (a s)"),
                                       xs[:, k, bass.ds(c * CK, CK)])
                ins.then_inc(stats, 1)

            def gate(n, part):
                first = (0, 3, R1, R2, R3)[part]
                count = [first]

                def link(ins):
                    count[0] += 1
                    ins.then_inc(step, 1)
                    dve.wait_ge(step, n * STEPS + count[0])

                if part == 0:
                    dve.wait_ge(stats, (n + 1) * NCK)
                    dve.memset(tick[:, 1:2], 0.0)
                    for k in range(KT):
                        ins = dve.bn_aggr(mv[:, k, :], bst[:, k, :, :])
                    link(ins)
                    dve.tensor_copy(me[:, 0, :], mean)
                    link(tt(sm[:, 0, :], mean, mean, ALU.mult))
                    link(tt(me[:, 1, :], sm[:, 0, :], var, ALU.add))
                elif part == 1:
                    dve.wait_ge(gp_done, n + 1)
                    link(dve.tensor_copy(gs[:].rearrange("p a k -> p (a k)"), psA[:, 0, 0:2 * KT]))
                    link(tt(sm[:, 1, :], gs[:, 0, :], gs[:, 0, :], ALU.mult))
                    link(tt(sm[:, 2, :], gs[:, 1, :], sm[:, 1, :], ALU.subtract))
                    link(ts_(sm[:, 3, :], sm[:, 2, :], EPS_GN, None, ALU.add))
                    assert count[0] == R1
                elif part == 2:
                    dve.wait_ge(root, 3 * n + 1)
                    link(dve.reciprocal(sm[:, 5, :], sm[:, 4, :]))
                    link(tt(sm[:, 0, :], var, sm[:, 5, :], ALU.mult))
                    link(tt(sm[:, 6, :], sm[:, 0, :], sm[:, 5, :], ALU.mult))
                    link(ts_(sm[:, 7, :], sm[:, 6, :], L / (L - 1.0), EPS_STD, ALU.mult, ALU.add))
                    assert count[0] == R2
                elif part == 3:
                    link(tt(sm[:, 0, :], mean, gs[:, 0, :], ALU.subtract))
                    link(tt(sm[:, 1, :], sm[:, 0, :], sm[:, 5, :], ALU.mult))
                    link(tt(sm[:, 2, :], sm[:, 1, :], pr[:, C_CFC0:C_CFC0 + KT], ALU.mult))
                    dve.wait_ge(root, 3 * n + 2)
                    link(tt(sm[:, 6, :], sm[:, 8, :], pr[:, C_CFC1:C_CFC1 + KT], ALU.mult))
                    link(tt(sm[:, 9, :], sm[:, 2, :], sm[:, 6, :], ALU.add))
                    assert count[0] == R3
                else:
                    dve.wait_ge(root, 3 * n + 3)
                    link(ts_(sm[:, 11, :], sm[:, 10, :], 1.0, None, ALU.add))
                    link(dve.reciprocal(sm[:, 0, :], sm[:, 11, :]))
                    link(tt(ab[:, 0, :], sm[:, 0, :], sm[:, 5, :], ALU.mult))
                    link(ts_(ab[:, 2, :], ab[:, 0, :], 1.0, None, ALU.add))
                    dve.scalar_tensor_tensor(out=ab[:, 1, :], in0=gs[:, 0, :], scalar=-1.0, in1=ab[:, 0, :],
                                             op0=ALU.mult, op1=ALU.mult).then_inc(ab_ready, 1)
                    assert count[0] == STEPS

            def evac(n, b, par, t, c):
                dve.wait_ge(scored, (n * NCK + b) * QT * NQ + t * NQ + c + 1)
                dve.tensor_scalar(cell(par, t, c), psA[:, c % 2, :], 1.0, None, ALU.mult, ALU.max,
                                  accum_out=mx[:, t, c:c + 1]).then_inc(a_used, 1)

            def neg_max(n, b, t):
                dve.wait_ge(a_used, a_idx(n, b, t, NQ))
                dve.tensor_reduce(nm[:, t:t + 1], mx[:, t, :], AX.X, ALU.max, negate=True).then_inc(negmax, 1)

            def low(out, ps, bias, high):
                if bias is None:
                    return dve.tensor_tensor(out, ps, high.bitcast(F32), ALU.subtract)
                return dve.scalar_tensor_tensor(out=out, in0=ps, scalar=bias, in1=high.bitcast(F32),
                                                op0=ALU.add, op1=ALU.subtract)

            def theta_l(n, b, slot):
                dve.wait_ge(thh_ready, n * NCK + b + 1)
                low(th_l[:], psT[:, slot, :], pr[:, C_THB:C_THB + 1], th_h[:]).then_inc(t_used, 1)

            def prob_l(n, b, e, j):
                dve.wait_ge(pTh_ready, (n * NCK + b) * JT + j + 1)
                low(pT_l[:, j % 4, :], psT[:, t_slot(e, j), :], None, pT_h[:, j % 4, :]).then_inc(t_used, 1)

            def inverse_sums(n, b, par):
                dve.wait_ge(exped, (n * NCK + b + 1) * QT * NQ)
                dve.tensor_reduce(dsum[:, 0, :], den[:, par, :, :], AX.X, ALU.add).then_inc(sums, 1)
                dve.wait_ge(sums, (n * NCK + b) * 2 + 1)
                dve.reciprocal(dsum[:, 1, :], dsum[:, 0, :]).then_inc(sums, 1)
                dve.wait_ge(sums, (n * NCK + b) * 2 + 2)
                for t in range(QT):
                    ins = dve.tensor_scalar(dg[:, t, :], ident[:], dsum[:, 1, t:t + 1], None, ALU.mult)
                ins.then_inc(dg_ready, 1)

            def stage(n, b, e, par, has_a, has_th):
                for j in range(JQ):
                    prob_l(n, b, e, j)
                for t in range(QT - 1):
                    for c in range(NQ):
                        if has_a:
                            evac(n, b + 1, 1 - par, t, c)
                        for j in range(JQ * (t + 1) + 2 * c, JQ * (t + 1) + 2 * c + 2):
                            prob_l(n, b, e, j)
                        if t == 1 and c == 0:
                            inverse_sums(n, b, par)
                        if not has_a:
                            if (t, c) == (0, 2):
                                chunk_stats(b)
                                gate(n + 1, 0)
                            elif (t, c) == (1, 1):
                                gate(n + 1, 1)
                            elif (t, c) == (1, 2):
                                gate(n + 1, 2)
                            elif (t, c) == (1, 3):
                                gate(n + 1, 3)
                            elif (t, c) == (2, 0):
                                dve.wait_ge(res_ready, n * NCK + b + 1)
                                gate(n + 1, 4)
                    if has_a:
                        neg_max(n, b + 1, t)
                if has_a:
                    evac(n, b + 1, 1 - par, QT - 1, 0)
                dve.wait_ge(pv_done, n * NCK + b + 1)
                dve.wait_ge(rb_ready, n * NCK + b + 1)
                dve.tensor_tensor(o_n[:], psO[:], rb[:], ALU.mult).then_inc(t_used, 1)
                if has_a:
                    for c in range(1, NQ):
                        evac(n, b + 1, 1 - par, QT - 1, c)
                    neg_max(n, b + 1, QT - 1)
                dve.wait_ge(res_ready, n * NCK + b + 1)
                for k in range(KT):
                    dve.wait_ge(t_ready, t_base(n, b) + T_OUT + k + 1)
                    dve.scalar_tensor_tensor(out=res[:, k, :], in0=psT[:, t_slot(e, T_OUT + k), :],
                                             scalar=pr[:, C_OUTB + k:C_OUTB + k + 1], in1=res[:, k, :],
                                             op0=ALU.add, op1=ALU.add).then_inc(t_used, 1)
                if has_a:
                    dve.wait_ge(x_loaded, 16 * KT * (n + 2))
                    chunk_stats(b)
                if has_th:
                    theta_l(n, b + 2, t_slot(e, T_TH))

            dve.wait_ge(consts, 3)
            dve.wait_ge(w_loaded, 80)
            dve.wait_ge(x_loaded, 16 * KT)
            for c in range(NCK):
                chunk_stats(c)
            for part in range(5):
                gate(0, part)
            with dve.Fori(0, N) as n:
                dve.wait_ge(ab_ready, n + 1)

                def s_chunk(c):
                    cols = slice(c * CK, (c + 1) * CK)
                    ts_(xs[:, 1, cols], xs[:, 1, cols], ab[:, 0, 1:2], ab[:, 1, 1:2],
                        ALU.mult, ALU.add).then_inc(s1_ready, 1)

                s_chunk(0)
                s_chunk(1)
                for c in range(NCK + 1):
                    if c == 2:
                        theta_l(n, 0, 0)
                    if c + 2 < NCK:
                        s_chunk(c + 2)
                    if c < NCK:
                        dve.wait_ge(phih_ready, n * NCK + c + 1)
                        low(phi_l[:, c * CK:(c + 1) * CK], psA[:, c % 2, 0:CK], pr[:, C_PHB:C_PHB + 1],
                            phi_h[:, c * CK:(c + 1) * CK]).then_inc(a_used, 1)
                    if c >= 1:
                        dve.wait_ge(gTh_ready, n * NCK + c)
                        js = slice((c - 1) * QT, c * QT)
                        low(gT_l[:, js, :], psO[:].rearrange("p (t q) -> p t q", t=QT), None,
                            gT_h[:, js, :]).then_inc(gTl_ready, 1)
                for t in range(QT):
                    for c in range(NQ):
                        evac(n, 0, 0, t, c)
                    neg_max(n, 0, t)
                theta_l(n, 1, 1)
                with dve.Fori(0, (NCK - 2) // 2) as pair:
                    for e in range(2):
                        stage(n, pair * 2 + e, 0, e, True, True)
                stage(n, NCK - 2, 0, 0, True, False)
                stage(n, NCK - 1, 1, 1, False, False)


R1, R2, R3, STEPS = 7, 11, 16, 20


def linear_attention_block(nc, x1, par, wqkv, wout, y):
    ctx = ExitStack()
    with ctx:
        def sb(name, shape, dt=F32):
            return ctx.enter_context(nc.sbuf_tensor("l1_" + name, shape, dt))

        def sem(name):
            return ctx.enter_context(nc.semaphore("l1_" + name))

        xb = sb("xb", [P, 2, KT, L])
        kraw = sb("kraw", [P, KT, L])
        vT = sb("vT", [P, JT, C])
        q = sb("q", [P, KT, L])
        tf = sb("tf", [P, KT, CK])
        t_h = sb("t_h", [P, 2, KT, CK], F32R)
        t_l = sb("t_l", [P, 2, KT, CK], F32R)
        wh = sb("wh", [P, KT, 3 * C], F32R)
        wl = sb("wl", [P, KT, 3 * C], F32R)
        wo = sb("wo", [P, KT, C])
        qs = sb("qs", [P, 2, 2, C])
        rq = sb("rq", [P, 2, 3, 2 * HEADS])
        kst = sb("kst", [P, KT, 2, NCK])
        kcol = sb("kcol", [P, 3, KT])
        cm = sb("cm", [P, KT, P])
        msum = sb("msum", [P, 2, KT])
        bc = sb("bc", [P, KT])
        pr = sb("pr", [P, N_PAR])
        ident = sb("ident", [P, P])
        omean = sb("omean", [P, P])
        grp = sb("grp", [P, P])
        tick = sb("tick", [P, 4])
        bst = sb("bst", [P, KT, NCK, 6])
        mv = sb("mv", [P, KT, 2])
        me = sb("me", [P, 2, KT])
        gs = sb("gs", [P, 2, KT])
        sm = sb("sm", [P, 6, KT])
        ab = sb("ab", [P, 2, KT])
        epsc = sb("epsc", [P, 1])

        wf = kraw[:, :, 0:3 * C]
        ke, kT = tf, qs[:].rearrange("p h t c -> p h (t c)")
        mTc = kraw[:, 0, 0:2 * C].rearrange("p (g o) -> p g o", g=KT)
        mT = kraw[:, 0, 2 * C:4 * C].rearrange("p (g o) -> p g o", g=KT)
        cT = kraw[:, 0, 4 * C:5 * C].rearrange("p (g o) -> p g o", g=KT)
        room = vT[:].rearrange("p j c -> p (j c)")
        sqr = room[:, 0:4 * CK].rearrange("p (a o c) -> p a o c", a=2, o=KT)
        yb = room[:, 4 * CK:8 * CK].rearrange("p (a o c) -> p a o c", a=2, o=KT)
        ssq = room[:, 8 * CK:10 * CK].rearrange("p (a c) -> p a c", a=2)
        logv = room[:, 10 * CK:12 * CK].rearrange("p (a c) -> p a c", a=2)
        rstd = room[:, 12 * CK:14 * CK].rearrange("p (a c) -> p a c", a=2)

        ps = ctx.enter_context(nc.psum_tensor("l1_ps", [P, 8, CK], F32))

        w_loaded = sem("w_loaded")
        x_loaded = [sem("x_loaded0"), sem("x_loaded1")]
        y_stored = sem("y_stored")
        const_step = sem("const_step")
        consts = sem("consts")
        wh_ready = sem("wh_ready")
        wl_ready = sem("wl_ready")
        b_mean = sem("b_mean")
        bc_ready = sem("bc_ready")
        stats = sem("stats")
        step = sem("step")
        root = sem("root")
        gp_done = sem("gp_done")
        t_normed = sem("t_normed")
        th_ready = sem("th_ready")
        tl_ready = sem("tl_ready")
        qv_mm = sem("qv_mm")
        k_mm = sem("k_mm")
        q_maxed = sem("q_maxed")
        q_shifted = sem("q_shifted")
        q_exped = sem("q_exped")
        v_copied = sem("v_copied")
        q_summed = sem("q_summed")
        q_inv = sem("q_inv")
        q_normed = sem("q_normed")
        q_turned = sem("q_turned")
        q_copied = sem("q_copied")
        k_copied = sem("k_copied")
        k_negmax = sem("k_negmax")
        k_exped = sem("k_exped")
        k_turned = sem("k_turned")
        kT_ready = sem("kT_ready")
        ctx_mm = sem("ctx_mm")
        m_step = sem("m_step")
        m_mm = sem("m_mm")
        y_mm = sem("y_mm")
        sq_ready = sem("sq_ready")
        ss_ready = sem("ss_ready")
        var_mm = sem("var_mm")
        log_ready = sem("log_ready")
        rstd_ready = sem("rstd_ready")
        yb_ready = sem("yb_ready")
        z_ready = sem("z_ready")
        y_ready = sem("y_ready")

        NP = NCK * 2
        NS = NCK * KT
        x1_v = x1.rearrange("n (k p) l -> n p k l", p=P)
        y_v = y.rearrange("n (k p) l -> n p k l", p=P)

        def chunk(c):
            return bass.ds(c * CK, CK)

        block = ctx.enter_context(nc.Block())

        @block.sync
        def _(sp):
            for dst, src in ((wf, wqkv.rearrange("(k p) o -> p k o", p=P)),
                             (wo[:], wout.rearrange("(k p) o -> p k o", p=P)), (pr[:], par[:, :])):
                sp.dma_start(dst, src).then_inc(w_loaded, 16)
            for n in range(2):
                for k in range(KT):
                    sp.dma_start(xb[:, n, k, :], x1_v[n, :, k, :]).then_inc(x_loaded[n], 16)
            for n in range(2, N):
                sp.wait_ge(y_stored, 16 * (NCK * (n - 1) + 1))
                for k in range(KT):
                    sp.dma_start(xb[:, n % 2, k, :], x1_v[n, :, k, :]).then_inc(x_loaded[n % 2], 16)
            sp.sem_inc(x_loaded[N % 2], 16 * KT)
            sp.wait_ge(y_stored, 16 * (NCK * N + 1))

        @block.gpsimd
        def _(pool):
            pool.memset(ident[:], 0.0).then_inc(const_step, 1)
            pool.memset(grp[:], 1.0 / GC).then_inc(const_step, 1)
            pool.memset(omean[:], 1.0 / C).then_inc(consts, 1)
            pool.memset(epsc[:], EPS_LN).then_inc(consts, 1)
            pool.memset(cm[:], 0.0).then_inc(consts, 1)
            for i, (s, count) in enumerate(((y_stored, 16), (yb_ready, 2), (log_ready, 2))):
                pool.memset(tick[:, i + 1:i + 2], 0.0).then_inc(s, count)
            pool.wait_ge(const_step, 2)
            pool.affine_select(out=ident[:], in_=ident[:], compare_op=ALU.not_equal, fill=1.0, base=0,
                               pattern=[[-1, P]], channel_multiplier=1).then_inc(consts, 1)
            gv = grp[:].rearrange("p (a c) -> p a c", c=GC)
            pool.affine_select(out=gv, in_=gv, compare_op=ALU.is_ge, fill=0.0, base=0,
                               pattern=[[-GC, P // GC], [0, GC]], channel_multiplier=1).then_inc(const_step, 1)
            pool.wait_ge(const_step, 3)
            pool.affine_select(out=gv, in_=gv, compare_op=ALU.is_ge, fill=0.0, base=GC - 1,
                               pattern=[[GC, P // GC], [0, GC]], channel_multiplier=-1).then_inc(consts, 1)

            def t_low(n, c, buf):
                pool.wait_ge(th_ready, n * NCK + c + 1)
                pool.tensor_tensor(t_l[:, buf, :, :], tf[:], t_h[:, buf, :, :].bitcast(F32),
                                   ALU.subtract).then_inc(tl_ready, 1)

            def q_norm(n, c, h):
                pool.wait_ge(q_inv, n * NP + c * 2 + h + 1)
                v = qs[:, h, :, :].rearrange("p t (a d) -> p (t a) d", d=DH)
                pool.tensor_tensor(v, v, rq[:, h, 2, :].unsqueeze(2).to_broadcast([P, 2 * HEADS, DH]),
                                   ALU.mult).then_inc(q_normed, 1)

            def chunk_qkv(n, c, buf, more):
                q_norm(n, c, 0)
                if more:
                    t_low(n, c + 1, 1 - buf)
                q_norm(n, c, 1)

            t_low(0, 0, 0)
            with pool.Fori(0, N) as n:
                with pool.Fori(0, NCK // 2 - 1) as pair:
                    for e in range(2):
                        chunk_qkv(n, pair * 2 + e, e, True)
                chunk_qkv(n, NCK - 2, 0, True)
                chunk_qkv(n, NCK - 1, 1, False)
                t_low(n + 1, 0, 0)
                with pool.Fori(0, NCK // 2) as pair:
                    for e in range(2):
                        pool.wait_ge(sq_ready, n * NCK + pair * 2 + e + 1)
                        pool.tensor_tensor(ssq[:, e, :], sqr[:, e, 0, :], sqr[:, e, 1, :],
                                           ALU.add).then_inc(ss_ready, 1)

        @block.tensor
        def _(pe):
            pe.wait_ge(consts, 5)
            pe.wait_ge(w_loaded, 48)
            for k in range(KT):
                ins = pe.matmul(ps[:, 0, 0:1], omean[:], pr[:, C_BOUT + k:C_BOUT + k + 1],
                                start=(k == 0), stop=(k == KT - 1))
            ins.then_inc(b_mean, 1)
            pe.wait_ge(wh_ready, KT)
            pe.wait_ge(wl_ready, KT)

            def qv(n, c, buf, h, first):
                if first:
                    pe.wait_ge(yb_ready, n * NCK + 1 + h)
                else:
                    pe.wait_ge(v_copied, n * NP + c * 2 + h - 1)
                for t in range(2):
                    at = slice((2 * h + t) * P, (2 * h + t + 1) * P)
                    for k in range(KT):
                        for i, (a, b) in enumerate(((t_h, wh), (t_l, wh), (t_h, wl))):
                            ins = pe.matmul(ps[:, 2 * h + t, :], a[:, buf, k, at], b[:, k, 0:2 * C],
                                            start=(k == 0 and i == 0), stop=(k == KT - 1 and i == 2))
                ins.then_inc(qv_mm, 1)

            def k_proj(n, c, buf, o, first):
                if first:
                    pe.wait_ge(log_ready, n * NCK + 1 + o)
                else:
                    pe.wait_ge(k_copied, n * NS + c * KT + o - 1)
                w = slice((4 + o) * P, (5 + o) * P)
                for k in range(KT):
                    for i, (a, b) in enumerate(((wh, t_h), (wl, t_h), (wh, t_l))):
                        ins = pe.matmul(ps[:, 4 + o, :], a[:, k, w], b[:, buf, k, :],
                                        start=(k == 0 and i == 0), stop=(k == KT - 1 and i == 2))
                ins.then_inc(k_mm, 1)

            def q_turn(n, c, h, first):
                pe.wait_ge(q_normed, n * NP + c * 2 + h + 1)
                if not first:
                    pe.wait_ge(q_copied, n * NP + c * 2 + h - 1)
                for o in range(KT):
                    for t in range(2):
                        ins = pe.transpose(ps[:, 6 + h, (2 * o + t) * P:(2 * o + t + 1) * P],
                                           qs[:, h, t, o * P:(o + 1) * P], ident[:])
                ins.then_inc(q_turned, 1)

            def chunk_qkv(n, c, buf, first, second=False):
                pe.wait_ge(tl_ready, n * NCK + c + 1)
                pe.wait_ge(th_ready, n * NCK + c + 1)
                qv(n, c, buf, 0, first)
                k_proj(n, c, buf, 0, first)
                if not first:
                    q_turn(n, c - 1, 1, second)
                qv(n, c, buf, 1, first)
                k_proj(n, c, buf, 1, first)
                q_turn(n, c, 0, first)

            def k_turn(n, c, o, first):
                pe.wait_ge(k_exped, n * NS + c * KT + o + 1)
                if not first:
                    pe.wait_ge(kT_ready, n * NS + c * KT + o - 1)
                for t in range(QT):
                    ins = pe.transpose(ps[:, 4 + o, t * P:(t + 1) * P], ke[:, o, t * P:(t + 1) * P], ident[:])
                ins.then_inc(k_turned, 1)

            def context(n, c, o, start, stop):
                pe.wait_ge(kT_ready, n * NS + c * KT + o + 1)
                for t in range(QT):
                    ins = pe.matmul(ps[:, 6 + o, 0:P], kT[:, o, t * P:(t + 1) * P],
                                    vT[:, c * QT + t, o * P:(o + 1) * P],
                                    start=(start and t == 0), stop=(stop and t == QT - 1),
                                    skip_group_check=True)
                ins.then_inc(ctx_mm, 1)

            def y_prod(n, c, par, first):
                if not first:
                    pe.wait_ge(yb_ready, n * NCK + c + 1)
                for o in range(KT):
                    for g in range(KT):
                        ins = pe.matmul(ps[:, 2 * par + o, :], mTc[:, g, o * P:(o + 1) * P], q[:, g, chunk(c)],
                                        start=(g == 0), stop=(g == KT - 1))
                ins.then_inc(y_mm, 1)

            def var(n, c, par):
                pe.wait_ge(ss_ready, n * NCK + c + 1)
                pe.matmul(ps[:, 4 + par, :], omean[:], ssq[:, par, :], start=True, stop=True).then_inc(var_mm, 1)

            def group_means(n):
                pe.wait_ge(step, n * G_STEPS + 3)
                pe.matmul(ps[:, 6, 0:2 * KT], grp[:], me[:].rearrange("p a k -> p (a k)"),
                          start=True, stop=True).then_inc(gp_done, 1)

            group_means(0)
            with pe.Fori(0, N) as n:
                chunk_qkv(n, 0, 0, True)
                chunk_qkv(n, 1, 1, False, True)
                with pe.Fori(1, NCK // 2) as pair:
                    for e in range(2):
                        chunk_qkv(n, pair * 2 + e, e, False)
                q_turn(n, NCK - 1, 1, False)
                for o in range(KT):
                    k_turn(n, 0, o, True)
                for o in range(KT):
                    k_turn(n, 1, o, False)
                    if o == 0:
                        pe.wait_ge(q_copied, (n + 1) * NP)
                    context(n, 0, o, True, False)
                with pe.Fori(2, NCK) as c:
                    for o in range(KT):
                        k_turn(n, c, o, False)
                        context(n, c - 1, o, False, False)
                for o in range(KT):
                    context(n, NCK - 1, o, False, True)
                pe.wait_ge(m_step, n * M_STEPS + 3)
                for g in range(KT):
                    ins = pe.transpose(ps[:, 0, g * P:(g + 1) * P], cm[:, g, :], ident[:])
                ins.then_inc(m_mm, 1)
                pe.wait_ge(m_step, n * M_STEPS + 4)
                for g in range(KT):
                    ins = pe.matmul(ps[:, 1, g * C:(g + 1) * C], cT[:, g, :], wo[:, g, :], start=True, stop=True)
                ins.then_inc(m_mm, 1)
                group_means(n + 1)
                pe.wait_ge(m_step, (n + 1) * M_STEPS)
                y_prod(n, 0, 0, True)
                y_prod(n, 1, 1, True)
                var(n, 0, 0)
                with pe.Fori(1, NCK // 2) as pair:
                    for e in range(2):
                        y_prod(n, pair * 2 + e, e, False)
                        var(n, pair * 2 + e - 1, 1 - e)
                var(n, NCK - 1, 1)

        @block.scalar
        def _(act):
            act.wait_ge(w_loaded, 48)
            for k in range(KT):
                act.activation(wh[:, k, 0:C], wf[:, k, 0:C], ACT.Copy)
                act.activation(wh[:, k, C:2 * C], wf[:, k, 2 * C:3 * C], ACT.Copy)
                act.activation(wh[:, k, 2 * C:3 * C], wf[:, k, C:2 * C], ACT.Copy).then_inc(wh_ready, 1)
            act.wait_ge(consts, 5)

            def t_high(n, c, buf):
                act.wait_ge(t_normed, n * NCK + c + 1)
                act.activation(t_h[:, buf, :, :], tf[:], ACT.Copy).then_inc(th_ready, 1)

            def q_exp(n, c, h):
                act.wait_ge(q_shifted, n * NP + c * 2 + h + 1)
                act.activation(qs[:, h, :, :], qs[:, h, :, :], ACT.Exp).then_inc(q_exped, 1)

            def v_copy(n, c, h):
                act.activation(vT[:, bass.ds(c * QT + 2 * h, 2), :], ps[:, 2 * h:2 * h + 2, C:2 * C],
                               ACT.Copy).then_inc(v_copied, 1)

            def q_copy(n, c, h):
                act.wait_ge(q_turned, n * NP + c * 2 + h + 1)
                act.activation(q[:, :, bass.ds(c * CK + h * 2 * P, 2 * P)],
                               ps[:, 6 + h, :].rearrange("p (o t) -> p o t", o=KT), ACT.Copy).then_inc(q_copied, 1)

            def chunk_qkv(n, c, buf, first, more):
                q_exp(n, c, 0)
                v_copy(n, c, 0)
                if more:
                    t_high(n, c + 1, 1 - buf)
                if not first:
                    q_copy(n, c - 1, 1)
                q_exp(n, c, 1)
                v_copy(n, c, 1)
                q_copy(n, c, 0)

            def k_exp(n, c, o, first):
                if not first:
                    act.wait_ge(k_turned, n * NS + c * KT + o - 1)
                act.activation(ke[:, o, :], kraw[:, o, chunk(c)], ACT.Exp, bias=kcol[:, 0, o:o + 1],
                               accum_out=kst[:, o, 1, bass.ds(c, 1)]).then_inc(k_exped, 1)

            def square(n, c, par):
                act.wait_ge(y_mm, n * NCK + c + 1)
                for o in range(KT):
                    ins = act.activation(sqr[:, par, o, :], ps[:, 2 * par + o, :], ACT.Square, bias=bc[:, o:o + 1])
                ins.then_inc(sq_ready, 1)

            def y_copy(n, c, par, first):
                if not first:
                    act.wait_ge(y_ready, n * NCK + c - 1)
                for o in range(KT):
                    ins = act.activation(yb[:, par, o, :], ps[:, 2 * par + o, :], ACT.Identity, bias=bc[:, o:o + 1])
                ins.then_inc(yb_ready, 1)

            def inverse_deviation(n, c, par):
                act.wait_ge(var_mm, n * NCK + c + 1)
                act.activation(logv[:, par, :], ps[:, 4 + par, :], ACT.Ln, bias=epsc[:, 0:1]).then_inc(log_ready, 1)
                act.wait_ge(log_ready, n * NCK + c + 3)
                act.activation(rstd[:, par, :], logv[:, par, :], ACT.Exp, scale=-0.5).then_inc(rstd_ready, 1)

            def store(n, c):
                act.wait_ge(y_ready, n * NCK + c + 1)
                act.dma_start(y_v[n, :, :, chunk(c)], xb[:, n % 2, :, chunk(c)]).then_inc(y_stored, 16)

            act.wait_ge(bc_ready, 2)

            def next_image(n):
                act.wait_ge(step, n * G_STEPS + G_ROOT)
                act.activation(sm[:, 4, :], sm[:, 3, :], ACT.Sqrt).then_inc(root, 1)
                act.preload_act_table_set("natural_log_exp_and_others")
                t_high(n, 0, 0)

            next_image(0)
            with act.Fori(0, N) as n:
                chunk_qkv(n, 0, 0, True, True)
                chunk_qkv(n, 1, 1, False, True)
                with act.Fori(1, NCK // 2 - 1) as pair:
                    for e in range(2):
                        chunk_qkv(n, pair * 2 + e, e, False, True)
                chunk_qkv(n, NCK - 2, 0, False, True)
                chunk_qkv(n, NCK - 1, 1, False, False)
                q_copy(n, NCK - 1, 1)
                act.wait_ge(k_negmax, n + 1)
                for o in range(KT):
                    k_exp(n, 0, o, True)
                with act.Fori(1, NCK) as c:
                    for o in range(KT):
                        k_exp(n, c, o, False)
                next_image(n + 1)
                act.wait_ge(y_stored, 16 * (n * NCK + 1))
                for e in range(2):
                    square(n, e, e)
                    y_copy(n, e, e, True)
                inverse_deviation(n, 0, 0)
                with act.Fori(1, NCK // 2) as pair:
                    for e in range(2):
                        square(n, pair * 2 + e, e)
                        y_copy(n, pair * 2 + e, e, False)
                        inverse_deviation(n, pair * 2 + e - 1, 1 - e)
                        store(n, pair * 2 + e - 2)
                inverse_deviation(n, NCK - 1, 1)
                store(n, NCK - 2)
                store(n, NCK - 1)

        @block.vector
        def _(dve):
            dve.wait_ge(w_loaded, 48)
            dve.wait_ge(consts, 5)
            dve.wait_ge(b_mean, 1)
            dve.tensor_copy(msum[:, 0, 0:1], ps[:, 0, 0:1]).then_inc(bc_ready, 1)
            dve.wait_ge(bc_ready, 1)
            dve.tensor_scalar(bc[:], pr[:, C_BOUT:C_BOUT + KT], msum[:, 0, 0:1], None,
                              ALU.subtract).then_inc(bc_ready, 1)
            for k in range(KT):
                dve.wait_ge(wh_ready, k + 1)
                for dst, src in ((0, 0), (C, 2 * C), (2 * C, C)):
                    ins = dve.tensor_tensor(wl[:, k, dst:dst + C], wf[:, k, src:src + C],
                                            wh[:, k, dst:dst + C].bitcast(F32), ALU.subtract)
                ins.then_inc(wl_ready, 1)

            def heads(ap):
                return ap.rearrange("p t (a d) -> p t a d", d=DH)

            def t_norm(n, c, half, first=False):
                if not first:
                    dve.wait_ge(tl_ready, n * NCK + c)
                for k in range(KT):
                    ins = dve.tensor_scalar(tf[:, k, :], xb[:, half, k, chunk(c)], ab[:, 0, k:k + 1],
                                            ab[:, 1, k:k + 1], ALU.mult, ALU.add)
                ins.then_inc(t_normed, 1)

            def q_shift(n, c, h):
                i = n * NP + c * 2 + h
                dve.wait_ge(qv_mm, i + 1)
                src = heads(ps[:, 2 * h:2 * h + 2, 0:C])
                dve.tensor_reduce(rq[:, h, 0, :], src, AX.X, ALU.max).then_inc(q_maxed, 1)
                dve.wait_ge(q_maxed, i + 1)
                dve.tensor_tensor(heads(qs[:, h, :, :]), src,
                                  rq[:, h, 0, :].rearrange("p (t a) -> p t a", t=2).unsqueeze(3)
                                  .to_broadcast([P, 2, HEADS, DH]), ALU.subtract).then_inc(q_shifted, 1)

            def q_sum(n, c, h):
                i = n * NP + c * 2 + h
                dve.wait_ge(q_exped, i + 1)
                dve.tensor_reduce(rq[:, h, 1, :], heads(qs[:, h, :, :]), AX.X, ALU.add).then_inc(q_summed, 1)
                dve.wait_ge(q_summed, i + 1)
                dve.reciprocal(rq[:, h, 2, :], rq[:, h, 1, :]).then_inc(q_inv, 1)

            def k_copy(n, c, o):
                dve.wait_ge(k_mm, n * NS + c * KT + o + 1)
                dve.tensor_scalar(kraw[:, o, chunk(c)], ps[:, 4 + o, :], 1.0, None, ALU.mult, ALU.max,
                                  accum_out=kst[:, o, 0, bass.ds(c, 1)]).then_inc(k_copied, 1)

            def kT_copy(n, c, o, first):
                if not first:
                    dve.wait_ge(ctx_mm, n * NS + c * KT + o - 1)
                dve.wait_ge(k_turned, n * NS + c * KT + o + 1)
                dve.tensor_copy(kT[:, o, :], ps[:, 4 + o, :]).then_inc(kT_ready, 1)

            def z_and_y(n, c, par, half):
                dve.wait_ge(rstd_ready, n * NCK + c + 1)
                for o in range(KT):
                    ins = tt(yb[:, par, o, :], yb[:, par, o, :], rstd[:, par, :], ALU.mult)
                ins.then_inc(z_ready, 1)
                dve.wait_ge(z_ready, n * NCK + c + 1)
                for o in range(KT):
                    at = xb[:, half, o, chunk(c)]
                    ins = dve.scalar_tensor_tensor(out=at, in0=yb[:, par, o, :], scalar=pr[:, C_LNG + o:C_LNG + o + 1],
                                                   in1=at, op0=ALU.mult, op1=ALU.add)
                ins.then_inc(y_ready, 1)

            tt = dve.tensor_tensor
            mean, var = mv[:, :, 0], mv[:, :, 1]

            class Steps:

                def __init__(self, sem, first, done=0):
                    self.sem, self.first, self.done = sem, first, done

                def __call__(self, ins):
                    self.done += 1
                    ins.then_inc(self.sem, 1)
                    dve.wait_ge(self.sem, self.first + self.done)

            def channel_means(n):
                link = Steps(step, n * G_STEPS)
                dve.wait_ge(stats, (n + 1) * NCK)
                dve.memset(tick[:, 0:1], 0.0)
                for k in range(KT):
                    ins = dve.bn_aggr(mv[:, k, :], bst[:, k, :, :])
                link(ins)
                dve.tensor_copy(me[:, 0, :], mean)
                link(tt(sm[:, 0, :], mean, mean, ALU.mult))
                link(tt(me[:, 1, :], sm[:, 0, :], var, ALU.add))

            def norm_columns(n):
                link = Steps(step, n * G_STEPS, 3)
                dve.wait_ge(gp_done, n + 1)
                link(dve.tensor_copy(gs[:].rearrange("p a k -> p (a k)"), ps[:, 6, 0:2 * KT]))
                link(tt(sm[:, 1, :], gs[:, 0, :], gs[:, 0, :], ALU.mult))
                link(tt(sm[:, 2, :], gs[:, 1, :], sm[:, 1, :], ALU.subtract))
                link(dve.tensor_scalar(sm[:, 3, :], sm[:, 2, :], EPS_GN, None, ALU.add))
                assert link.done == G_ROOT
                dve.wait_ge(root, n + 1)
                link(dve.reciprocal(ab[:, 0, :], sm[:, 4, :]))
                link(dve.scalar_tensor_tensor(out=ab[:, 1, :], in0=gs[:, 0, :], scalar=-1.0, in1=ab[:, 0, :],
                                              op0=ALU.mult, op1=ALU.mult))
                assert link.done == G_STEPS

            def chunk_stats(c, buf):
                for k in range(KT):
                    ins = dve.bn_stats(bst[:, k, bass.ds(c, 1), :].rearrange("p a s -> p (a s)"),
                                       xb[:, buf, k, chunk(c)])
                ins.then_inc(stats, 1)

            dve.wait_ge(x_loaded[0], 16 * KT)
            for c in range(NCK):
                chunk_stats(c, 0)
            channel_means(0)
            norm_columns(0)
            t_norm(0, 0, 0, True)
            with dve.Fori(0, N // 2) as two:
              for half in range(2):
                n = two * 2 + half

                def chunk_qk(c):
                    q_shift(n, c, 0)
                    k_copy(n, c, 0)
                    q_sum(n, c, 0)
                    q_shift(n, c, 1)
                    k_copy(n, c, 1)
                    q_sum(n, c, 1)

                with dve.Fori(0, NCK - 1) as c:
                    t_norm(n, c + 1, half)
                    chunk_qk(c)
                chunk_qk(NCK - 1)
                dve.wait_ge(k_copied, (n + 1) * NS)
                dve.tensor_reduce(kcol[:, 0, :], kst[:, :, 0, :], AX.X, ALU.max, negate=True).then_inc(k_negmax, 1)
                dve.wait_ge(x_loaded[1 - half], two * 16 * KT + 16 * KT * (1 + half))
                for o in range(KT):
                    kT_copy(n, 0, o, True)
                chunk_stats(0, 1 - half)
                with dve.Fori(1, NCK) as c:
                    for o in range(KT):
                        kT_copy(n, c, o, False)
                    chunk_stats(c, 1 - half)
                channel_means(n + 1)
                mlink = Steps(m_step, n * M_STEPS)
                dve.wait_ge(k_exped, (n + 1) * NS)
                mlink(dve.tensor_reduce(kcol[:, 1, :], kst[:, :, 1, :], AX.X, ALU.add))
                mlink(dve.reciprocal(kcol[:, 2, :], kcol[:, 1, :]))
                dve.wait_ge(ctx_mm, (n + 1) * NS)
                for g in range(KT):
                    for a in range(P // DH):
                        r = slice(a * DH, (a + 1) * DH)
                        ins = dve.tensor_scalar(cm[r, g, r], ps[r, 6 + g, r], DH ** -0.5 / L, None, ALU.mult)
                mlink(ins)
                dve.wait_ge(m_mm, 2 * n + 1)
                mlink(dve.tensor_copy(kraw[:, 0, 4 * C:5 * C], ps[:, 0, 0:KT * P]))
                dve.wait_ge(m_mm, 2 * n + 2)
                for g in range(KT):
                    ins = dve.tensor_scalar(mT[:, g, :], ps[:, 1, g * C:(g + 1) * C], kcol[:, 2, g:g + 1], None,
                                            ALU.mult)
                mlink(ins)
                mlink(dve.tensor_reduce(msum[:, 0, :], mT, AX.X, ALU.add))
                mlink(dve.tensor_scalar(msum[:, 1, :], msum[:, 0, :], -1.0 / C, None, ALU.mult))
                for g in range(KT):
                    ins = dve.tensor_scalar(mTc[:, g, :], mT[:, g, :], msum[:, 1, g:g + 1], None, ALU.add)
                ins.then_inc(m_step, 1)
                norm_columns(n + 1)
                t_norm(n + 1, 0, 1 - half, True)
                with dve.Fori(0, NCK // 2) as pair:
                    for e in range(2):
                        z_and_y(n, pair * 2 + e, e, half)


G_ROOT, G_STEPS, M_STEPS = 7, 9, 8


def program(nc, x, par, wth, wph, wg, wout, wqkv, wo, y):
    x1 = nc.dram_tensor("x1_between", [N, C, L], F32, kind="Internal").ap()
    nonlocal_block(nc, x, par, wth, wph, wg, wout, x1)
    linear_attention_block(nc, x1, par, wqkv, wo, y)


def kernel(**inputs):
    import numpy as np
    import concourse.bacc as bacc
    from concourse.bass_utils import run_bass_kernel_spmd

    def columns(a):
        return np.asarray(a).reshape(-1, P).T

    i = {name: np.asarray(a) for name, a in inputs.items()}
    par = np.concatenate([columns(a) for a in (
        i["L0_conv_cfc"][:, 0], i["L0_conv_cfc"][:, 1], i["L0_conv_theta_b"], i["L0_conv_phi_b"], i["L0_conv_g_b"],
        i["L0_conv_out_b"], i["L1_conv_b_out"], i["L1_conv_g"])], axis=1)
    arrays = {"x": i["x"].reshape(N, C, L), "par": par, "wth": i["L0_conv_theta_w"].T, "wph": i["L0_conv_phi_w"].T,
              "wg": i["L0_conv_g_w"].T, "wout": i["L0_conv_out_w"].T, "wqkv": i["L1_conv_w_qkv"].T,
              "wo": i["L1_conv_w_out"].T}
    nc = bacc.Bacc("TRN2", target_bir_lowering=False, num_devices=1)
    fed, args = {}, []
    for name, a in arrays.items():
        fed[f"in_{name}"] = np.ascontiguousarray(a)
        args.append(nc.dram_tensor(f"in_{name}", a.shape, mybir.dt.from_np(a.dtype), kind="ExternalInput").ap())
    args.append(nc.dram_tensor("out_y", [N, C, L], F32, kind="ExternalOutput").ap())
    program(nc, *args)
    r = run_bass_kernel_spmd(nc, [fed], core_ids=[0])
    return r.results[0]["out_y"].reshape(N, C, 64, 64)
```

```python
from contextlib import ExitStack

import concourse.bass as bass
from concourse import mybir

ALU = mybir.AluOpType
ACT = mybir.ActivationFunctionType
F32 = mybir.dt.float32
F32R = mybir.dt.float32r
AX = mybir.AxisListType

P = 128
N, C, L = 4, 256, 4096
KT = C // P
CH = C // 2
CK = 512
NCK = L // CK
QT = CK // P
NQ = 4
QW = L // NQ
JQ = QW // P
JT = L // P
GROUPS = 32
GC = C // GROUPS
PIECES = 4
EPS_GN = 1e-5
EPS_STD = 1e-5
EPS_LN = 1e-5
HEADS, DH = 8, 32

C_CFC0, C_CFC1, C_THB, C_PHB, C_GB, C_OUTB, C_BOUT, C_LNG = 0, 2, 4, 5, 6, 7, 9, 11
N_PAR = 13


def nonlocal_block(nc, x, par, wth, wph, wg, wout, x1):
    ctx = ExitStack()
    with ctx:
        def sb(name, shape, dt=F32):
            return ctx.enter_context(nc.sbuf_tensor(name, shape, dt))

        def sem(name):
            return ctx.enter_context(nc.semaphore(name))

        probs = sb("probs", [P, QT * NQ, QW])
        phi_h = sb("phi_h", [P, L], F32R)
        phi_l = sb("phi_l", [P, L], F32R)
        gT_h = sb("gT_h", [P, JT, P], F32R)
        gT_l = sb("gT_l", [P, JT, P], F32R)
        xs = sb("xs", [P, KT, L])
        pT_h = sb("pT_h", [P, 4, CK], F32R)
        pT_l = sb("pT_l", [P, 4, CK], F32R)
        th_h = sb("th_h", [P, CK], F32R)
        th_l = sb("th_l", [P, CK], F32R)
        sq = sb("sq", [P, KT, CK])
        res = sb("res", [P, KT, CK])
        o_n = sb("o_n", [P, CK])
        rb = sb("rb", [P, CK])
        dg_h = sb("dg_h", [P, QT, P], F32R)
        dg_l = sb("dg_l", [P, QT, P], F32R)
        wth_s = sb("wth_s", [P, KT, CH])
        wph_h = sb("wph_h", [P, KT, CH], F32R)
        wph_l = sb("wph_l", [P, KT, CH], F32R)
        wg_h = sb("wg_h", [P, KT, CH], F32R)
        wg_l = sb("wg_l", [P, KT, CH], F32R)
        wout_s = sb("wout_s", [P, C])
        pr = sb("pr", [P, N_PAR])
        ident = sb("ident", [P, P])
        ones = sb("ones", [P, P], F32R)
        grp = sb("grp", [P, P])
        tick = sb("tick", [P, 3])
        bst = sb("bst", [P, KT, NCK, 6])
        mv = sb("mv", [P, KT, 2])
        me = sb("me", [P, 2, KT])
        gs = sb("gs", [P, 2, KT])
        sm = sb("sm", [P, 12, KT])
        ab = sb("ab", [P, 3, KT])
        mx = sb("mx", [P, QT, NQ])
        nm = sb("nm", [P, QT])
        den = sb("den", [P, 2, QT, NQ])
        dsum = sb("dsum", [P, 2, QT])

        def of_phi(buf, i):
            return buf[:, i * KT * CK:(i + 1) * KT * CK].rearrange("p (k c) -> p k c", k=KT)

        def of_gT(buf, i):
            tiles = KT * QT
            return buf[:, i * tiles:(i + 1) * tiles, :].rearrange("p (k t) q -> p k (t q)", k=KT)

        def of_pT(buf, i):
            return buf[:, KT * i:KT * (i + 1), :]

        s_h = [of_phi(phi_h, 2), of_phi(phi_h, 3), of_phi(phi_l, 2), of_phi(phi_l, 3),
               of_phi(phi_h, 3), of_pT(pT_h, 0), of_pT(pT_h, 1), of_gT(gT_l, 3)]
        s_l = [of_gT(gT_h, 0), of_gT(gT_h, 1), of_gT(gT_l, 2), of_gT(gT_l, 3),
               of_gT(gT_h, 3), of_pT(pT_l, 0), of_pT(pT_l, 1), of_gT(gT_h, 3)]
        wph_s, wg_s = (probs[:, 12, i * KT * CH:(i + 1) * KT * CH].rearrange("p (k c) -> p k c", k=KT)
                       for i in range(2))

        psA = ctx.enter_context(nc.psum_tensor("psA", [P, 2, 2 * CK], F32))
        psT = ctx.enter_context(nc.psum_tensor("psT", [P, 3, CK], F32))
        psO = ctx.enter_context(nc.psum_tensor("psO", [P, CK], F32))

        w_loaded = sem("w_loaded")
        x_piece = [sem(f"x_piece{i}") for i in range(PIECES)]
        x_loaded = sem("x_loaded")
        sq_loaded = sem("sq_loaded")
        res_loaded = sem("res_loaded")
        res_free = sem("res_free")
        consts = sem("consts")
        const_step = sem("const_step")
        gp_done = sem("gp_done")
        stats = sem("stats")
        step = sem("step")
        root = sem("root")
        ab_ready = sem("ab_ready")
        wh_ready = sem("wh_ready")
        wl_ready = sem("wl_ready")
        s_ready = sem("s_ready")
        sh_ready = sem("sh_ready")
        sl_ready = sem("sl_ready")
        sq_ready = sem("sq_ready")
        res_ready = sem("res_ready")
        phi_mm = sem("phi_mm")
        g_mm = sem("g_mm")
        g_copied = sem("g_copied")
        phih_ready = sem("phih_ready")
        g_turned = sem("g_turned")
        gTh_ready = sem("gTh_ready")
        gTl_ready = sem("gTl_ready")
        scored = sem("scored")
        a_used = sem("a_used")
        negmax = sem("negmax")
        exped = sem("exped")
        t_ready = sem("t_ready")
        t_used = sem("t_used")
        pTh_ready = sem("pTh_ready")
        th_mm = sem("th_mm")
        thh_ready = sem("thh_ready")
        thl_ready = sem("thl_ready")
        out_mm = sem("out_mm")
        sums = sem("sums")
        dg_ready = sem("dg_ready")
        rb_ready = sem("rb_ready")
        pv_done = sem("pv_done")

        A_BLOCK = QT * NQ + 2
        A_IMG = NCK + NCK * A_BLOCK + 2

        def a_idx(n, b, t, c):
            return n * A_IMG + NCK + b * A_BLOCK + t * NQ + c

        def a_tail(n, b):
            behind_scores = 0 if isinstance(b, int) and b == NCK - 1 else QT * NQ
            return n * A_IMG + NCK + (b + 1) * A_BLOCK + behind_scores

        def read(uses):
            return uses + 2

        T_STAGE = JT + 1
        T_IMG = NCK * T_STAGE
        T_INV = JT
        assert T_STAGE % 3 == 0

        def t_base(n, b):
            return n * T_IMG + b * T_STAGE

        def used(uses):
            return uses + 3

        def turned(c):
            return psO[:, :] if c % 2 == 0 else psT[:, 1, :]

        def out_tile(k, has_th):
            return psA[:, 1, k * CK:(k + 1) * CK] if has_th else psA[:, k, 0:CK]

        def cell(par, t, q):
            return probs[:, (t * NQ + q) if par == 0 else (q * NQ + t), :]

        x_v = x.rearrange("n (k p) l -> n p k l", p=P)
        x1_v = x1.rearrange("n (k p) l -> n p k l", p=P)
        block = ctx.enter_context(nc.Block())

        @block.sync
        def _(sp):
            for i in range(PIECES):
                cols = slice(i * (L // PIECES), (i + 1) * (L // PIECES))
                sp.dma_start(xs[:, :, cols], x_v[0, :, :, cols]).then_inc(x_piece[i], 16)
            for dst, src in ((wth_s[:], wth.rearrange("(k p) o -> p k o", p=P)),
                             (wph_s, wph.rearrange("(k p) o -> p k o", p=P)),
                             (wg_s, wg.rearrange("(k p) o -> p k o", p=P)),
                             (wout_s[:], wout[:, :]), (pr[:], par[:, :])):
                sp.dma_start(dst, src).then_inc(w_loaded, 16)

            def stage(n, b, has_th):
                sp.wait_ge(res_free, 16 * (n * NCK + b + 1))
                sp.dma_start(res[:], x_v[n, :, :, bass.ds(b * CK, CK)]).then_inc(res_loaded, 16)
                if has_th:
                    sp.wait_ge(th_mm, n * NCK + b + 2)
                    sp.dma_start(sq[:], x_v[n, :, :, bass.ds((b + 2) * CK, CK)]).then_inc(sq_loaded, 16)
                sp.wait_ge(a_used, read(a_tail(n, b) + 2))
                sp.dma_start(x1_v[n, :, :, bass.ds(b * CK, CK)], res[:]).then_inc(res_free, 16)

            def load_x(n):
                for k in range(KT):
                    sp.dma_start(xs[:, k, :], x_v[n, :, k, :]).then_inc(x_loaded, 16)

            def image(n, last):
                sp.dma_start(sq[:], x_v[n, :, :, 0:CK]).then_inc(sq_loaded, 16)
                sp.wait_ge(th_mm, n * NCK + 1)
                sp.dma_start(sq[:], x_v[n, :, :, CK:2 * CK]).then_inc(sq_loaded, 16)
                sp.wait_ge(phi_mm, (n + 1) * NCK)
                if last:
                    sp.sem_inc(x_loaded, 16 * KT)
                else:
                    load_x(n + 1)
                with sp.Fori(0, (NCK - 2) // 2) as pair:
                    for e in range(2):
                        stage(n, pair * 2 + e, True)
                stage(n, NCK - 2, False)
                stage(n, NCK - 1, False)

            with sp.Fori(0, N - 1) as n:
                image(n, False)
            image(N - 1, True)
            sp.wait_ge(res_free, 16 * (N * NCK + 1))

        @block.gpsimd
        def _(pool):
            pool.memset(ident[:], 0.0).then_inc(const_step, 1)
            pool.memset(rb[:, 0:P], 1.0).then_inc(consts, 1)
            pool.memset(tick[:, 0:1], 0.0).then_inc(res_free, 16)
            pool.memset(tick[:, 1:2], 0.0).then_inc(t_used, 3)
            pool.memset(tick[:, 2:3], 0.0).then_inc(a_used, 2)
            pool.memset(grp[:], 1.0 / GC).then_inc(const_step, 1)
            pool.wait_ge(const_step, 2)
            pool.affine_select(out=ident[:], in_=ident[:], compare_op=ALU.not_equal, fill=1.0, base=0,
                               pattern=[[-1, P]], channel_multiplier=1).then_inc(consts, 1)
            gv = grp[:].rearrange("p (a c) -> p a c", c=GC)
            pool.affine_select(out=gv, in_=gv, compare_op=ALU.is_ge, fill=0.0, base=0,
                               pattern=[[-GC, P // GC], [0, GC]], channel_multiplier=1).then_inc(const_step, 1)
            pool.wait_ge(const_step, 3)
            pool.affine_select(out=gv, in_=gv, compare_op=ALU.is_ge, fill=0.0, base=GC - 1,
                               pattern=[[GC, P // GC], [0, GC]], channel_multiplier=-1).then_inc(consts, 1)

            def carry(i):
                pool.tensor_tensor(tick[:, i:i + 1], ab[:, 0, 0:1], ab[:, 0, 0:1], ALU.add)

            def s_block(n, b):
                pool.wait_ge(sq_loaded, 16 * (n * NCK + b + 1))
                carry(0)
                for k in range(KT):
                    ins = pool.tensor_scalar(sq[:, k, :], sq[:, k, :], ab[:, 0, k:k + 1], ab[:, 1, k:k + 1],
                                             ALU.mult, ALU.add)
                ins.then_inc(sq_ready, 1)

            def s_chunk(n, c):
                cols = slice(c * CK, (c + 1) * CK)
                for k in range(KT):
                    ins = pool.tensor_scalar(xs[:, k, cols], xs[:, k, cols], ab[:, 0, k:k + 1], ab[:, 1, k:k + 1],
                                             ALU.mult, ALU.add)
                ins.then_inc(s_ready, 1)

            def stage(n, b, has_th):
                pool.wait_ge(res_loaded, 16 * (n * NCK + b + 1))
                carry(2)
                for k in range(KT):
                    ins = pool.tensor_scalar(res[:, k, :], res[:, k, :], ab[:, 2, k:k + 1], ab[:, 1, k:k + 1],
                                             ALU.mult, ALU.add)
                ins.then_inc(res_ready, 1)
                if has_th:
                    s_block(n, b + 2)

            def first_chunks(n):
                pool.wait_ge(ab_ready, n + 1)
                carry(1)
                s_chunk(n, 0)
                s_chunk(n, 1)

            first_chunks(0)
            with pool.Fori(0, N) as n:
                for c in range(2, NCK):
                    s_chunk(n, c)
                    if c == 3:
                        s_block(n, 0)
                s_block(n, 1)
                with pool.Fori(0, (NCK - 2) // 2) as pair:
                    for e in range(2):
                        stage(n, pair * 2 + e, True)
                stage(n, NCK - 2, False)
                stage(n, NCK - 1, False)
                first_chunks(n + 1)

        @block.tensor
        def _(pe):
            pe.wait_ge(consts, 3)
            pe.wait_ge(w_loaded, 80)

            def three_pass(out, lh, ll, rh, rl, start, stop):
                pe.matmul(out, lh, rh, start=start, stop=False)
                pe.matmul(out, ll, rh, start=False, stop=False)
                return pe.matmul(out, lh, rl, start=False, stop=stop)

            def theta(n, b, out):
                pe.wait_ge(sq_ready, n * NCK + b + 1)
                for k in range(KT):
                    ins = pe.matmul(out, wth_s[:, k, :], sq[:, k, :], start=(k == 0), stop=(k == KT - 1))
                ins.then_inc(th_mm, 1)

            def scores(n, b, t, c):
                pe.wait_ge(a_used, read(a_idx(n, b, t, c) - 1))
                for h in range(2):
                    cols = slice(c * QW + h * CK, c * QW + (h + 1) * CK)
                    q = slice(t * P, (t + 1) * P)
                    ins = three_pass(psA[:, c % 2, h * CK:(h + 1) * CK], th_h[:, q], th_l[:, q],
                                     phi_h[:, cols], phi_l[:, cols], True, True)
                ins.then_inc(scored, 1)

            def turn(n, b, e, par, j):
                base = t_base(n, b)
                if j % JQ == 0:
                    pe.wait_ge(exped, (n * NCK + b + 1) * QT * NQ - NQ + j // JQ + 1)
                pe.wait_ge(t_used, used(base + j - 2))
                for t in range(QT):
                    ins = pe.transpose(psT[:, j % 3, t * P:(t + 1) * P],
                                       cell(par, t, j // JQ)[:, (j % JQ) * P:(j % JQ + 1) * P], ident[:])
                ins.then_inc(t_ready, 1)

            def weigh(n, b, j):
                pe.wait_ge(t_used, used(t_base(n, b) + j + 1))
                s = j % 4
                ins = three_pass(psO[:, :], gT_h[:, j, :], gT_l[:, j, :], pT_h[:, s, :], pT_l[:, s, :],
                                 j == 0, j == JT - 1)
                if j == JT - 1:
                    ins.then_inc(pv_done, 1)

            def group_means(n):
                pe.wait_ge(step, n * STEPS + 3)
                pe.matmul(psA[:, 0, 0:2 * KT], grp[:], me[:].rearrange("p a k -> p (a k)"),
                          start=True, stop=True).then_inc(gp_done, 1)

            def stage(n, b, e, par, has_a, has_th):
                base = t_base(n, b)
                for j in range(1, JQ):
                    turn(n, b, e, par, j)
                    if j >= 2:
                        weigh(n, b, j - 2)
                for t in range(QT - 1):
                    for c in range(NQ):
                        if has_a:
                            scores(n, b + 1, t, c)
                        elif (t, c) == (1, 0):
                            group_means(n + 1)
                        for j in range(JQ * (t + 1) + 2 * c, JQ * (t + 1) + 2 * c + 2):
                            turn(n, b, e, par, j)
                            weigh(n, b, j - 2)
                pe.wait_ge(dg_ready, n * NCK + b + 1)
                pe.wait_ge(t_used, used(base + T_INV - 2))
                pe.matmul(psT[:, T_INV % 3, :], ones[:], dg_h[:].rearrange("p t q -> p (t q)"),
                          start=True, stop=False)
                pe.matmul(psT[:, T_INV % 3, :], ones[:], dg_l[:].rearrange("p t q -> p (t q)"),
                          start=False, stop=True).then_inc(t_ready, 1)
                if has_a:
                    scores(n, b + 1, QT - 1, 0)
                weigh(n, b, JT - 2)
                if has_a:
                    scores(n, b + 1, QT - 1, 1)
                    scores(n, b + 1, QT - 1, 2)
                weigh(n, b, JT - 1)
                if has_a:
                    scores(n, b + 1, QT - 1, 3)
                tail = a_tail(n, b)
                if has_th:
                    pe.wait_ge(a_used, read(tail - 1))
                    theta(n, b + 2, psA[:, 0, 0:CK])
                pe.wait_ge(t_used, used(base + T_INV + 1))
                for k in range(KT):
                    if has_th:
                        if k == 0:
                            pe.wait_ge(a_used, read(tail))
                    else:
                        pe.wait_ge(a_used, read(tail - 1 + k))
                    pe.matmul(out_tile(k, has_th), wout_s[:, k * P:(k + 1) * P], o_n[:],
                              start=True, stop=True).then_inc(out_mm, 1)
                    if has_a and k == (0 if has_th else 1):
                        turn(n, b + 1, 1 - e, 1 - par, 0)

            group_means(0)
            pe.wait_ge(wh_ready, 1)
            pe.wait_ge(wl_ready, 1)
            with pe.Fori(0, N) as n:
                for c in range(NCK + 1):
                    if c == 3:
                        theta(n, 0, psT[:, 0, :])
                    if c < NCK:
                        pe.wait_ge(sh_ready, n * NCK + c + 1)
                        pe.wait_ge(sl_ready, n * NCK + c + 1)
                        pe.wait_ge(a_used, read(n * A_IMG + c - 1))
                        for w_h, w_l, half, done in ((wg_h, wg_l, 1, g_mm), (wph_h, wph_l, 0, phi_mm)):
                            for k in range(KT):
                                ins = three_pass(psA[:, c % 2, half * CK:(half + 1) * CK], w_h[:, k, :], w_l[:, k, :],
                                                 s_h[c][:, k, :], s_l[c][:, k, :], k == 0, k == KT - 1)
                            ins.then_inc(done, 1)
                    if c >= 1:
                        pe.wait_ge(g_copied, n * NCK + c)
                        if c >= 3:
                            pe.wait_ge(gTl_ready, n * NCK + c - 2)
                        for t in range(QT):
                            ins = pe.transpose(turned(c - 1)[:, t * P:(t + 1) * P],
                                               probs[:, (c - 1) % 2, t * P:(t + 1) * P], ident[:])
                        ins.then_inc(g_turned, 1)
                pe.wait_ge(thl_ready, n + 1)
                for t in range(QT):
                    for c in range(NQ):
                        scores(n, 0, t, c)
                pe.wait_ge(gTl_ready, (n + 1) * NCK)
                pe.wait_ge(a_used, read(a_idx(n, 0, QT, 0) - 1))
                theta(n, 1, psA[:, 0, 0:CK])
                turn(n, 0, 0, 0, 0)
                with pe.Fori(0, (NCK - 2) // 2) as pair:
                    for e in range(2):
                        stage(n, pair * 2 + e, 0, e, True, True)
                stage(n, NCK - 2, 0, 0, True, False)
                stage(n, NCK - 1, 1, 1, False, False)

        @block.scalar
        def _(act):
            def exp(n, b, par, t, c):
                if c == 0:
                    act.wait_ge(negmax, (n * NCK + b) * QT + t + 1)
                act.activation(cell(par, t, c), cell(par, t, c), ACT.Exp, bias=nm[:, t:t + 1],
                               accum_out=den[:, par, t, c:c + 1]).then_inc(exped, 1)

            def gate_root(n, i):
                src, dst, func, scale, at = ((3, 4, ACT.Sqrt, 1.0, R1), (7, 8, ACT.Sqrt, 1.0, R2),
                                             (9, 10, ACT.Exp, -1.0, R3))[i]
                act.wait_ge(step, n * STEPS + at)
                act.activation(sm[:, dst, :], sm[:, src, :], func, scale=scale).then_inc(root, 1)

            def s_high(n, c):
                act.wait_ge(s_ready, n * NCK + c + 1)
                act.activation(s_h[c], xs[:, :, c * CK:(c + 1) * CK], ACT.Copy).then_inc(sh_ready, 1)

            def theta_h(n, b, src):
                act.wait_ge(th_mm, n * NCK + b + 1)
                act.activation(th_h[:], src, ACT.Identity,
                               bias=pr[:, C_THB:C_THB + 1]).then_inc(thh_ready, 1)

            def prob_h(n, b, e, j):
                act.wait_ge(t_ready, t_base(n, b) + j + 1)
                act.activation(pT_h[:, j % 4, :], psT[:, j % 3, :], ACT.Copy).then_inc(pTh_ready, 1)

            def stage(n, b, e, par, has_a, has_th):
                for j in range(JQ):
                    prob_h(n, b, e, j)
                    if j % 2 == 0 and j > 0:
                        exp(n, b, par, QT - 1, j // 2)
                for t in range(QT - 1):
                    for c in range(NQ):
                        if has_a and t >= 1:
                            exp(n, b + 1, 1 - par, t - 1, c)
                        for j in range(JQ * (t + 1) + 2 * c, JQ * (t + 1) + 2 * c + 2):
                            prob_h(n, b, e, j)
                        if not has_a and t == 1 and c >= 1:
                            gate_root(n + 1, c - 1)
                        if not has_a and t == 2 and c >= 2:
                            s_high(n + 1, c - 2)
                act.wait_ge(t_ready, t_base(n, b) + T_INV + 1)
                act.activation(rb[:], psT[:, T_INV % 3, :], ACT.Copy).then_inc(rb_ready, 1)
                if has_a:
                    for c in range(NQ):
                        exp(n, b + 1, 1 - par, QT - 2, c)
                    exp(n, b + 1, 1 - par, QT - 1, 0)
                if has_th:
                    theta_h(n, b + 2, psA[:, 0, 0:CK])

            act.wait_ge(w_loaded, 80)
            for i in range(3):
                gate_root(0, i)
            act.wait_ge(consts, 3)
            act.activation(ones[:], rb[:, 0:P], ACT.Copy)
            act.activation(wph_h[:], wph_s, ACT.Copy)
            act.activation(wg_h[:], wg_s, ACT.Copy).then_inc(wh_ready, 1)
            s_high(0, 0)
            s_high(0, 1)
            with act.Fori(0, N) as n:
                for c in range(NCK + 1):
                    if c == 3:
                        theta_h(n, 0, psT[:, 0, :])
                    if c + 2 < NCK:
                        s_high(n, c + 2)
                    if c < NCK:
                        act.wait_ge(g_mm, n * NCK + c + 1)
                        act.activation(probs[:, c % 2, 0:CK], psA[:, c % 2, CK:2 * CK], ACT.Identity,
                                       bias=pr[:, C_GB:C_GB + 1]).then_inc(g_copied, 1)
                        act.wait_ge(phi_mm, n * NCK + c + 1)
                        act.activation(phi_h[:, c * CK:(c + 1) * CK], psA[:, c % 2, 0:CK], ACT.Identity,
                                       bias=pr[:, C_PHB:C_PHB + 1]).then_inc(phih_ready, 1)
                    if c >= 1:
                        act.wait_ge(g_turned, n * NCK + c)
                        act.activation(gT_h[:, (c - 1) * QT:c * QT, :],
                                       turned(c - 1).rearrange("p (t q) -> p t q", t=QT), ACT.Copy).then_inc(gTh_ready, 1)
                for t in range(QT - 1):
                    for c in range(NQ):
                        exp(n, 0, 0, t, c)
                exp(n, 0, 0, QT - 1, 0)
                theta_h(n, 1, psA[:, 0, 0:CK])
                with act.Fori(0, (NCK - 2) // 2) as pair:
                    for e in range(2):
                        stage(n, pair * 2 + e, 0, e, True, True)
                stage(n, NCK - 2, 0, 0, True, False)
                stage(n, NCK - 1, 1, 1, False, False)

        @block.vector
        def _(dve):
            tt, ts_ = dve.tensor_tensor, dve.tensor_scalar
            mean, var = mv[:, :, 0], mv[:, :, 1]

            def channel_stats(c, k):
                return dve.bn_stats(bst[:, k, bass.ds(c, 1), :].rearrange("p a s -> p (a s)"),
                                    xs[:, k, bass.ds(c * CK, CK)])

            def chunk_stats(c):
                channel_stats(c, 0)
                channel_stats(c, 1).then_inc(stats, 1)

            def gate(n, part):
                first = (0, 3, R1, R2, R3)[part]
                count = [first]

                def link(ins):
                    count[0] += 1
                    ins.then_inc(step, 1)
                    dve.wait_ge(step, n * STEPS + count[0])

                if part == 0:
                    dve.wait_ge(stats, (n + 1) * NCK)
                    dve.memset(tick[:, 1:2], 0.0)
                    for k in range(KT):
                        ins = dve.bn_aggr(mv[:, k, :], bst[:, k, :, :])
                    link(ins)
                    dve.tensor_copy(me[:, 0, :], mean)
                    link(tt(sm[:, 0, :], mean, mean, ALU.mult))
                    link(tt(me[:, 1, :], sm[:, 0, :], var, ALU.add))
                elif part == 1:
                    dve.wait_ge(gp_done, n + 1)
                    link(dve.tensor_copy(gs[:].rearrange("p a k -> p (a k)"), psA[:, 0, 0:2 * KT]))
                    link(tt(sm[:, 1, :], gs[:, 0, :], gs[:, 0, :], ALU.mult))
                    link(tt(sm[:, 2, :], gs[:, 1, :], sm[:, 1, :], ALU.subtract))
                    link(ts_(sm[:, 3, :], sm[:, 2, :], EPS_GN, None, ALU.add))
                    assert count[0] == R1
                elif part == 2:
                    dve.wait_ge(root, 3 * n + 1)
                    link(dve.reciprocal(sm[:, 5, :], sm[:, 4, :]))
                    link(tt(sm[:, 0, :], var, sm[:, 5, :], ALU.mult))
                    link(tt(sm[:, 6, :], sm[:, 0, :], sm[:, 5, :], ALU.mult))
                    link(ts_(sm[:, 7, :], sm[:, 6, :], L / (L - 1.0), EPS_STD, ALU.mult, ALU.add))
                    assert count[0] == R2
                elif part == 3:
                    link(tt(sm[:, 0, :], mean, gs[:, 0, :], ALU.subtract))
                    link(tt(sm[:, 1, :], sm[:, 0, :], sm[:, 5, :], ALU.mult))
                    link(tt(sm[:, 2, :], sm[:, 1, :], pr[:, C_CFC0:C_CFC0 + KT], ALU.mult))
                    dve.wait_ge(root, 3 * n + 2)
                    link(tt(sm[:, 6, :], sm[:, 8, :], pr[:, C_CFC1:C_CFC1 + KT], ALU.mult))
                    link(tt(sm[:, 9, :], sm[:, 2, :], sm[:, 6, :], ALU.add))
                    assert count[0] == R3
                else:
                    dve.wait_ge(root, 3 * n + 3)
                    link(ts_(sm[:, 11, :], sm[:, 10, :], 1.0, None, ALU.add))
                    link(dve.reciprocal(sm[:, 0, :], sm[:, 11, :]))
                    link(tt(ab[:, 0, :], sm[:, 0, :], sm[:, 5, :], ALU.mult))
                    link(ts_(ab[:, 2, :], ab[:, 0, :], 1.0, None, ALU.add))
                    dve.scalar_tensor_tensor(out=ab[:, 1, :], in0=gs[:, 0, :], scalar=-1.0, in1=ab[:, 0, :],
                                             op0=ALU.mult, op1=ALU.mult).then_inc(ab_ready, 1)
                    assert count[0] == STEPS

            def s_low(n, c):
                dve.wait_ge(sh_ready, n * NCK + c + 1)
                tt(s_l[c], xs[:, :, c * CK:(c + 1) * CK], s_h[c].bitcast(F32),
                   ALU.subtract).then_inc(sl_ready, 1)

            def evac(n, b, par, t, c):
                dve.wait_ge(scored, (n * NCK + b) * QT * NQ + t * NQ + c + 1)
                dve.tensor_scalar(cell(par, t, c), psA[:, c % 2, :], 1.0, None, ALU.mult, ALU.max,
                                  accum_out=mx[:, t, c:c + 1]).then_inc(a_used, 1)

            def neg_max(n, b, t):
                dve.wait_ge(a_used, read(a_idx(n, b, t, NQ)))
                dve.tensor_reduce(nm[:, t:t + 1], mx[:, t, :], AX.X, ALU.max, negate=True).then_inc(negmax, 1)

            def low(out, ps, bias, high):
                if bias is None:
                    return dve.tensor_tensor(out, ps, high.bitcast(F32), ALU.subtract)
                return dve.scalar_tensor_tensor(out=out, in0=ps, scalar=bias, in1=high.bitcast(F32),
                                                op0=ALU.add, op1=ALU.subtract)

            def theta_l(n, b, src, done, count):
                dve.wait_ge(thh_ready, n * NCK + b + 1)
                low(th_l[:], src, pr[:, C_THB:C_THB + 1], th_h[:]).then_inc(done, count)

            def prob_l(n, b, e, j):
                dve.wait_ge(pTh_ready, (n * NCK + b) * JT + j + 1)
                low(pT_l[:, j % 4, :], psT[:, j % 3, :], None, pT_h[:, j % 4, :]).then_inc(t_used, 1)

            def inverse_sums(n, b, par):
                dve.wait_ge(exped, (n * NCK + b + 1) * QT * NQ)
                dve.tensor_reduce(dsum[:, 0, :], den[:, par, :, :], AX.X, ALU.add).then_inc(sums, 1)
                dve.wait_ge(sums, (n * NCK + b) * 3 + 1)
                dve.reciprocal(dsum[:, 1, :], dsum[:, 0, :]).then_inc(sums, 1)
                dve.wait_ge(sums, (n * NCK + b) * 3 + 2)
                for t in range(QT):
                    ins = dve.tensor_scalar(dg_h[:, t, :], ident[:], dsum[:, 1, t:t + 1], None, ALU.mult)
                ins.then_inc(sums, 1)
                dve.wait_ge(sums, (n * NCK + b) * 3 + 3)
                for t in range(QT):
                    ins = dve.scalar_tensor_tensor(out=dg_l[:, t, :], in0=ident[:], scalar=dsum[:, 1, t:t + 1],
                                                   in1=dg_h[:, t, :].bitcast(F32), op0=ALU.mult, op1=ALU.subtract)
                ins.then_inc(dg_ready, 1)

            def stage(n, b, e, par, has_a, has_th):
                for j in range(1, JQ):
                    prob_l(n, b, e, j)
                for t in range(QT - 1):
                    for c in range(NQ):
                        if has_a:
                            evac(n, b + 1, 1 - par, t, c)
                        for j in range(JQ * (t + 1) + 2 * c, JQ * (t + 1) + 2 * c + 2):
                            prob_l(n, b, e, j)
                        if t == 1 and c == 0:
                            inverse_sums(n, b, par)
                        if has_a and (t, c) == (1, 1):
                            dve.wait_ge(x_loaded, 16 * KT * (n + 1))
                            channel_stats(b, 0)
                        if has_a and (t, c) == (1, 3):
                            channel_stats(b, 1).then_inc(stats, 1)
                        if not has_a:
                            if (t, c) == (0, 2):
                                chunk_stats(b)
                                gate(n + 1, 0)
                            elif (t, c) == (1, 1):
                                gate(n + 1, 1)
                            elif (t, c) == (1, 2):
                                gate(n + 1, 2)
                            elif (t, c) == (1, 3):
                                gate(n + 1, 3)
                            elif (t, c) == (2, 0):
                                dve.wait_ge(res_ready, n * NCK + b + 1)
                                gate(n + 1, 4)
                            elif t == 2 and c >= 2:
                                s_low(n + 1, c - 2)
                    if has_a:
                        neg_max(n, b + 1, t)
                if has_a:
                    for c in range(NQ - 1):
                        evac(n, b + 1, 1 - par, QT - 1, c)
                dve.wait_ge(pv_done, n * NCK + b + 1)
                dve.wait_ge(rb_ready, n * NCK + b + 1)
                dve.tensor_tensor(o_n[:], psO[:], rb[:], ALU.mult).then_inc(t_used, 1)
                if has_a:
                    evac(n, b + 1, 1 - par, QT - 1, NQ - 1)
                    neg_max(n, b + 1, QT - 1)
                dve.wait_ge(res_ready, n * NCK + b + 1)
                for k in range(KT):
                    if has_th and k == 1:
                        theta_l(n, b + 2, psA[:, 0, 0:CK], a_used, 1)
                    if has_a and k == 1:
                        prob_l(n, b + 1, 1 - e, 0)
                    dve.wait_ge(out_mm, (n * NCK + b) * KT + k + 1)
                    ins = dve.scalar_tensor_tensor(out=res[:, k, :], in0=out_tile(k, has_th),
                                                   scalar=pr[:, C_OUTB + k:C_OUTB + k + 1], in1=res[:, k, :],
                                                   op0=ALU.add, op1=ALU.add)
                    if k == 1 or not has_th:
                        ins.then_inc(a_used, 1)

            dve.wait_ge(consts, 3)
            for c in range(NCK):
                if c % (NCK // PIECES) == 0:
                    dve.wait_ge(x_piece[c // (NCK // PIECES)], 16)
                chunk_stats(c)
            dve.wait_ge(w_loaded, 80)
            for part in range(5):
                gate(0, part)
            dve.wait_ge(wh_ready, 1)
            tt(wph_l[:], wph_s, wph_h[:].bitcast(F32), ALU.subtract)
            tt(wg_l[:], wg_s, wg_h[:].bitcast(F32), ALU.subtract).then_inc(wl_ready, 1)
            s_low(0, 0)
            s_low(0, 1)
            with dve.Fori(0, N) as n:
                for c in range(NCK + 1):
                    if c == 3:
                        theta_l(n, 0, psT[:, 0, :], thl_ready, 1)
                    if c + 2 < NCK:
                        s_low(n, c + 2)
                    if c < NCK:
                        dve.wait_ge(phih_ready, n * NCK + c + 1)
                        low(phi_l[:, c * CK:(c + 1) * CK], psA[:, c % 2, 0:CK], pr[:, C_PHB:C_PHB + 1],
                            phi_h[:, c * CK:(c + 1) * CK]).then_inc(a_used, 1)
                    if c >= 1:
                        dve.wait_ge(gTh_ready, n * NCK + c)
                        js = slice((c - 1) * QT, c * QT)
                        low(gT_l[:, js, :], turned(c - 1).rearrange("p (t q) -> p t q", t=QT), None,
                            gT_h[:, js, :]).then_inc(gTl_ready, 1)
                for t in range(QT):
                    for c in range(NQ):
                        evac(n, 0, 0, t, c)
                    neg_max(n, 0, t)
                theta_l(n, 1, psA[:, 0, 0:CK], a_used, 2)
                prob_l(n, 0, 0, 0)
                with dve.Fori(0, (NCK - 2) // 2) as pair:
                    for e in range(2):
                        stage(n, pair * 2 + e, 0, e, True, True)
                stage(n, NCK - 2, 0, 0, True, False)
                stage(n, NCK - 1, 1, 1, False, False)


R1, R2, R3, STEPS = 7, 11, 16, 20


def linear_attention_block(nc, x1, par, wqkv, wout, y):
    ctx = ExitStack()
    with ctx:
        def sb(name, shape, dt=F32):
            return ctx.enter_context(nc.sbuf_tensor("l1_" + name, shape, dt))

        def sem(name):
            return ctx.enter_context(nc.semaphore("l1_" + name))

        xb = sb("xb", [P, 2, KT, L])
        kraw = sb("kraw", [P, KT, L])
        vT = sb("vT", [P, JT, C])
        q = sb("q", [P, KT, L])
        tf = sb("tf", [P, KT, CK])
        t_h = sb("t_h", [P, 2, KT, CK], F32R)
        t_l = sb("t_l", [P, 2, KT, CK], F32R)
        wh = sb("wh", [P, KT, 3 * C], F32R)
        wl = sb("wl", [P, KT, 3 * C], F32R)
        wo = sb("wo", [P, KT, C])
        kT = sb("kT", [P, KT, CK])
        qs = sb("qs", [P, 2, 2, C])
        rq = sb("rq", [P, 2, 3, 2 * HEADS])
        kst = sb("kst", [P, KT, 2, NCK])
        kcol = sb("kcol", [P, 3, KT])
        cm = sb("cm", [P, KT, P])
        wsum = sb("wsum", [P, 2, KT])
        bsum = sb("bsum", [P, 1])
        bc = sb("bc", [P, KT])
        pr = sb("pr", [P, N_PAR])
        ident = sb("ident", [P, P])
        omean = sb("omean", [P, P])
        grp = sb("grp", [P, P])
        tick = sb("tick", [P, 4])
        bst = sb("bst", [P, KT, NCK, 6])
        mv = sb("mv", [P, KT, 2])
        me = sb("me", [P, 2, KT])
        gs = sb("gs", [P, 2, KT])
        sm = sb("sm", [P, 6, KT])
        ab = sb("ab", [P, 2, KT])
        epsc = sb("epsc", [P, 1])

        wf = kraw[:, :, 0:3 * C]
        ke = tf
        mT = kraw[:, 0, 0:2 * C].rearrange("p (g o) -> p g o", g=KT)
        cT = kraw[:, 0, 4 * C:5 * C].rearrange("p (g o) -> p g o", g=KT)
        room = vT[:].rearrange("p j c -> p (j c)")
        sqr = room[:, 0:4 * CK].rearrange("p (a o c) -> p a o c", a=2, o=KT)
        yb = room[:, 4 * CK:8 * CK].rearrange("p (a o c) -> p a o c", a=2, o=KT)
        ssq = room[:, 8 * CK:10 * CK].rearrange("p (a c) -> p a c", a=2)
        logv = room[:, 10 * CK:12 * CK].rearrange("p (a c) -> p a c", a=2)
        rstd = room[:, 12 * CK:14 * CK].rearrange("p (a c) -> p a c", a=2)

        ps = ctx.enter_context(nc.psum_tensor("l1_ps", [P, 8, CK], F32))

        w_loaded = sem("w_loaded")
        x_piece = [sem(f"x_piece{i}") for i in range(PIECES)]
        x_loaded = [sem("x_loaded0"), sem("x_loaded1")]
        y_stored = sem("y_stored")
        const_step = sem("const_step")
        consts = sem("consts")
        wh_ready = sem("wh_ready")
        wl_ready = sem("wl_ready")
        b_mean = sem("b_mean")
        bc_ready = sem("bc_ready")
        wo_step = sem("wo_step")
        stats = sem("stats")
        step = sem("step")
        root = sem("root")
        gp_done = sem("gp_done")
        t_normed = sem("t_normed")
        th_ready = sem("th_ready")
        tl_ready = sem("tl_ready")
        qv_mm = sem("qv_mm")
        k_mm = sem("k_mm")
        q_maxed = sem("q_maxed")
        q_shifted = sem("q_shifted")
        q_exped = sem("q_exped")
        v_copied = sem("v_copied")
        q_summed = sem("q_summed")
        q_inv = sem("q_inv")
        q_normed = sem("q_normed")
        q_turned = sem("q_turned")
        q_copied = sem("q_copied")
        k_copied = sem("k_copied")
        k_negmax = sem("k_negmax")
        k_exped = sem("k_exped")
        k_turned = sem("k_turned")
        kT_ready = sem("kT_ready")
        ctx_mm = sem("ctx_mm")
        m_step = sem("m_step")
        m_mm = sem("m_mm")
        y_mm = sem("y_mm")
        sq_ready = sem("sq_ready")
        ss_ready = sem("ss_ready")
        var_mm = sem("var_mm")
        log_ready = sem("log_ready")
        rstd_ready = sem("rstd_ready")
        yb_ready = sem("yb_ready")
        z_ready = sem("z_ready")
        y_ready = sem("y_ready")

        NP = NCK * 2
        NS = NCK * KT
        x1_v = x1.rearrange("n (k p) l -> n p k l", p=P)
        y_v = y.rearrange("n (k p) l -> n p k l", p=P)

        def chunk(c):
            return bass.ds(c * CK, CK)

        block = ctx.enter_context(nc.Block())

        @block.sync
        def _(sp):
            for i in range(PIECES):
                cols = slice(i * (L // PIECES), (i + 1) * (L // PIECES))
                sp.dma_start(xb[:, 0, :, cols], x1_v[0, :, :, cols]).then_inc(x_piece[i], 16)
            for dst, src in ((wf, wqkv.rearrange("(k p) o -> p k o", p=P)),
                             (wo[:], wout.rearrange("(k p) o -> p k o", p=P)), (pr[:], par[:, :])):
                sp.dma_start(dst, src).then_inc(w_loaded, 16)
            for k in range(KT):
                sp.dma_start(xb[:, 1, k, :], x1_v[1, :, k, :]).then_inc(x_loaded[1], 16)
            for n in range(2, N):
                sp.wait_ge(y_stored, 16 * (NCK * (n - 1) + 1))
                for k in range(KT):
                    sp.dma_start(xb[:, n % 2, k, :], x1_v[n, :, k, :]).then_inc(x_loaded[n % 2], 16)
            sp.sem_inc(x_loaded[N % 2], 16 * KT)
            sp.wait_ge(y_stored, 16 * (NCK * N + 1))

        @block.gpsimd
        def _(pool):
            pool.memset(ident[:], 0.0).then_inc(const_step, 1)
            pool.memset(grp[:], 1.0 / GC).then_inc(const_step, 1)
            pool.memset(omean[:], 1.0 / C).then_inc(consts, 1)
            pool.memset(epsc[:], EPS_LN).then_inc(consts, 1)
            pool.memset(cm[:], 0.0).then_inc(consts, 1)
            for i, (s, count) in enumerate(((y_stored, 16), (yb_ready, 2), (log_ready, 2))):
                pool.memset(tick[:, i + 1:i + 2], 0.0).then_inc(s, count)
            pool.wait_ge(const_step, 2)
            pool.affine_select(out=ident[:], in_=ident[:], compare_op=ALU.not_equal, fill=1.0, base=0,
                               pattern=[[-1, P]], channel_multiplier=1).then_inc(consts, 1)
            gv = grp[:].rearrange("p (a c) -> p a c", c=GC)
            pool.affine_select(out=gv, in_=gv, compare_op=ALU.is_ge, fill=0.0, base=0,
                               pattern=[[-GC, P // GC], [0, GC]], channel_multiplier=1).then_inc(const_step, 1)
            pool.wait_ge(const_step, 3)
            pool.affine_select(out=gv, in_=gv, compare_op=ALU.is_ge, fill=0.0, base=GC - 1,
                               pattern=[[GC, P // GC], [0, GC]], channel_multiplier=-1).then_inc(consts, 1)

            def t_low(n, c, buf):
                pool.wait_ge(th_ready, n * NCK + c + 1)
                pool.tensor_tensor(t_l[:, buf, :, :], tf[:], t_h[:, buf, :, :].bitcast(F32),
                                   ALU.subtract).then_inc(tl_ready, 1)

            def q_norm(n, c, h):
                pool.wait_ge(q_inv, n * NP + c * 2 + h + 1)
                v = qs[:, h, :, :].rearrange("p t (a d) -> p (t a) d", d=DH)
                pool.tensor_tensor(v, v, rq[:, h, 2, :].unsqueeze(2).to_broadcast([P, 2 * HEADS, DH]),
                                   ALU.mult).then_inc(q_normed, 1)

            def chunk_qkv(n, c, buf, more):
                if more:
                    t_low(n, c + 1, 1 - buf)
                q_norm(n, c, 0)
                q_norm(n, c, 1)

            t_low(0, 0, 0)
            with pool.Fori(0, N) as n:
                t_low(n, 1, 1)
                chunk_qkv(n, 0, 0, False)
                chunk_qkv(n, 1, 1, True)
                with pool.Fori(1, NCK // 2 - 1) as pair:
                    for e in range(2):
                        chunk_qkv(n, pair * 2 + e, e, True)
                chunk_qkv(n, NCK - 2, 0, True)
                chunk_qkv(n, NCK - 1, 1, False)
                t_low(n + 1, 0, 0)
                with pool.Fori(0, NCK // 2) as pair:
                    for e in range(2):
                        pool.wait_ge(sq_ready, n * NCK + pair * 2 + e + 1)
                        pool.tensor_tensor(ssq[:, e, :], sqr[:, e, 0, :], sqr[:, e, 1, :],
                                           ALU.add).then_inc(ss_ready, 1)

        @block.tensor
        def _(pe):
            def group_means(n):
                pe.wait_ge(step, n * G_STEPS + 3)
                pe.matmul(ps[:, 6, 0:2 * KT], grp[:], me[:].rearrange("p a k -> p (a k)"),
                          start=True, stop=True).then_inc(gp_done, 1)

            pe.wait_ge(consts, 5)
            group_means(0)
            pe.wait_ge(w_loaded, 48)
            for k in range(KT):
                ins = pe.matmul(ps[:, 0, 0:1], omean[:], pr[:, C_BOUT + k:C_BOUT + k + 1],
                                start=(k == 0), stop=(k == KT - 1))
            ins.then_inc(b_mean, 1)
            pe.wait_ge(wh_ready, KT)
            pe.wait_ge(wl_ready, KT)

            def qv(n, c, buf, h, first):
                if first:
                    pe.wait_ge(yb_ready, n * NCK + 1 + h)
                else:
                    pe.wait_ge(v_copied, n * NP + c * 2 + h - 1)
                for t in range(2):
                    at = slice((2 * h + t) * P, (2 * h + t + 1) * P)
                    for k in range(KT):
                        for i, (a, b) in enumerate(((t_h, wh), (t_l, wh), (t_h, wl))):
                            ins = pe.matmul(ps[:, 2 * h + t, :], a[:, buf, k, at], b[:, k, 0:2 * C],
                                            start=(k == 0 and i == 0), stop=(k == KT - 1 and i == 2))
                ins.then_inc(qv_mm, 1)

            def k_proj(n, c, buf, o, first):
                if first:
                    pe.wait_ge(log_ready, n * NCK + 1 + o)
                else:
                    pe.wait_ge(k_copied, n * NS + c * KT + o - 1)
                w = slice((4 + o) * P, (5 + o) * P)
                for k in range(KT):
                    for i, (a, b) in enumerate(((wh, t_h), (wl, t_h), (wh, t_l))):
                        ins = pe.matmul(ps[:, 4 + o, :], a[:, k, w], b[:, buf, k, :],
                                        start=(k == 0 and i == 0), stop=(k == KT - 1 and i == 2))
                ins.then_inc(k_mm, 1)

            def q_turn(n, c, h, first):
                pe.wait_ge(q_normed, n * NP + c * 2 + h + 1)
                if not first:
                    pe.wait_ge(q_copied, n * NP + c * 2 + h - 1)
                for o in range(KT):
                    for t in range(2):
                        ins = pe.transpose(ps[:, 6 + h, (2 * o + t) * P:(2 * o + t + 1) * P],
                                           qs[:, h, t, o * P:(o + 1) * P], ident[:])
                ins.then_inc(q_turned, 1)

            def chunk_qkv(n, c, buf, first, second=False):
                pe.wait_ge(tl_ready, n * NCK + c + 1)
                pe.wait_ge(th_ready, n * NCK + c + 1)
                qv(n, c, buf, 0, first)
                k_proj(n, c, buf, 0, first)
                if not first:
                    q_turn(n, c - 1, 1, second)
                qv(n, c, buf, 1, first)
                k_proj(n, c, buf, 1, first)
                q_turn(n, c, 0, first)

            def k_turn(n, c, o, first):
                pe.wait_ge(k_exped, n * NS + c * KT + o + 1)
                if not first:
                    pe.wait_ge(kT_ready, n * NS + c * KT + o - 1)
                for t in range(QT):
                    ins = pe.transpose(ps[:, 4 + o, t * P:(t + 1) * P], ke[:, o, t * P:(t + 1) * P], ident[:])
                ins.then_inc(k_turned, 1)

            def context(n, c, o, start, stop):
                pe.wait_ge(kT_ready, n * NS + c * KT + o + 1)
                for t in range(QT):
                    ins = pe.matmul(ps[:, 6 + o, 0:P], kT[:, o, t * P:(t + 1) * P],
                                    vT[:, c * QT + t, o * P:(o + 1) * P],
                                    start=(start and t == 0), stop=(stop and t == QT - 1),
                                    skip_group_check=True)
                ins.then_inc(ctx_mm, 1)

            def y_prod(n, c, par, first):
                if not first:
                    pe.wait_ge(yb_ready, n * NCK + c + 1)
                for o in range(KT):
                    for g in range(KT):
                        ins = pe.matmul(ps[:, 2 * par + o, :], mT[:, g, o * P:(o + 1) * P], q[:, g, chunk(c)],
                                        start=(g == 0), stop=(g == KT - 1))
                ins.then_inc(y_mm, 1)

            def var(n, c, par):
                pe.wait_ge(ss_ready, n * NCK + c + 1)
                pe.matmul(ps[:, 4 + par, :], omean[:], ssq[:, par, :], start=True, stop=True).then_inc(var_mm, 1)

            with pe.Fori(0, N) as n:
                chunk_qkv(n, 0, 0, True)
                chunk_qkv(n, 1, 1, False, True)
                with pe.Fori(1, NCK // 2) as pair:
                    for e in range(2):
                        chunk_qkv(n, pair * 2 + e, e, False)
                for o in range(KT):
                    k_turn(n, 0, o, True)
                for o in range(KT):
                    k_turn(n, 1, o, False)
                    if o == 0:
                        q_turn(n, NCK - 1, 1, False)
                    if o == 0:
                        pe.wait_ge(q_copied, (n + 1) * NP)
                    context(n, 0, o, True, False)
                with pe.Fori(2, NCK) as c:
                    for o in range(KT):
                        k_turn(n, c, o, False)
                        context(n, c - 1, o, False, False)
                for o in range(KT):
                    context(n, NCK - 1, o, False, True)
                pe.wait_ge(m_step, n * M_STEPS + 3)
                for g in range(KT):
                    ins = pe.transpose(ps[:, 0, g * P:(g + 1) * P], cm[:, g, :], ident[:])
                ins.then_inc(m_mm, 1)
                pe.wait_ge(m_step, n * M_STEPS + 4)
                pe.wait_ge(wo_step, 3)
                for g in range(KT):
                    ins = pe.matmul(ps[:, 1, g * C:(g + 1) * C], cT[:, g, :], wo[:, g, :], start=True, stop=True)
                ins.then_inc(m_mm, 1)
                group_means(n + 1)
                pe.wait_ge(m_step, (n + 1) * M_STEPS)
                y_prod(n, 0, 0, True)
                y_prod(n, 1, 1, True)
                var(n, 0, 0)
                with pe.Fori(1, NCK // 2) as pair:
                    for e in range(2):
                        y_prod(n, pair * 2 + e, e, False)
                        var(n, pair * 2 + e - 1, 1 - e)
                var(n, NCK - 1, 1)

        @block.scalar
        def _(act):
            act.wait_ge(w_loaded, 48)
            for k in range(KT):
                act.activation(wh[:, k, 0:C], wf[:, k, 0:C], ACT.Copy)
                act.activation(wh[:, k, C:2 * C], wf[:, k, 2 * C:3 * C], ACT.Copy)
                act.activation(wh[:, k, 2 * C:3 * C], wf[:, k, C:2 * C], ACT.Copy).then_inc(wh_ready, 1)
            act.wait_ge(consts, 5)

            def t_high(n, c, buf):
                act.wait_ge(t_normed, n * NCK + c + 1)
                act.activation(t_h[:, buf, :, :], tf[:], ACT.Copy).then_inc(th_ready, 1)

            def q_exp(n, c, h):
                act.wait_ge(q_shifted, n * NP + c * 2 + h + 1)
                act.activation(qs[:, h, :, :], qs[:, h, :, :], ACT.Exp).then_inc(q_exped, 1)

            def v_copy(n, c, h):
                act.activation(vT[:, bass.ds(c * QT + 2 * h, 2), :], ps[:, 2 * h:2 * h + 2, C:2 * C],
                               ACT.Copy).then_inc(v_copied, 1)

            def q_copy(n, c, h):
                act.wait_ge(q_turned, n * NP + c * 2 + h + 1)
                act.activation(q[:, :, bass.ds(c * CK + h * 2 * P, 2 * P)],
                               ps[:, 6 + h, :].rearrange("p (o t) -> p o t", o=KT), ACT.Copy).then_inc(q_copied, 1)

            def chunk_qkv(n, c, buf, first, more):
                if more and not first:
                    t_high(n, c + 1, 1 - buf)
                q_exp(n, c, 0)
                v_copy(n, c, 0)
                if not first:
                    q_copy(n, c - 1, 1)
                if not more:
                    k_exp(n, 0, 0, True)
                q_exp(n, c, 1)
                v_copy(n, c, 1)
                q_copy(n, c, 0)

            def k_exp(n, c, o, first):
                if first:
                    act.wait_ge(k_negmax, n * KT + o + 1)
                else:
                    act.wait_ge(k_turned, n * NS + c * KT + o - 1)
                act.activation(ke[:, o, :], kraw[:, o, chunk(c)], ACT.Exp, bias=kcol[:, 0, o:o + 1],
                               accum_out=kst[:, o, 1, bass.ds(c, 1)]).then_inc(k_exped, 1)

            def square(n, c, par):
                act.wait_ge(y_mm, n * NCK + c + 1)
                for o in range(KT):
                    ins = act.activation(sqr[:, par, o, :], ps[:, 2 * par + o, :], ACT.Square, bias=bc[:, o:o + 1])
                ins.then_inc(sq_ready, 1)

            def y_copy(n, c, par, first):
                if not first:
                    act.wait_ge(y_ready, n * NCK + c - 1)
                for o in range(KT):
                    ins = act.activation(yb[:, par, o, :], ps[:, 2 * par + o, :], ACT.Identity, bias=bc[:, o:o + 1])
                ins.then_inc(yb_ready, 1)

            def inverse_deviation(n, c, par):
                act.wait_ge(var_mm, n * NCK + c + 1)
                act.activation(logv[:, par, :], ps[:, 4 + par, :], ACT.Ln, bias=epsc[:, 0:1]).then_inc(log_ready, 1)
                act.wait_ge(log_ready, n * NCK + c + 3)
                act.activation(rstd[:, par, :], logv[:, par, :], ACT.Exp, scale=-0.5).then_inc(rstd_ready, 1)

            def store(n, c):
                act.wait_ge(y_ready, n * NCK + c + 1)
                act.dma_start(y_v[n, :, :, chunk(c)], xb[:, n % 2, :, chunk(c)]).then_inc(y_stored, 16)

            def next_image(n):
                act.wait_ge(step, n * G_STEPS + G_ROOT)
                act.activation(sm[:, 4, :], sm[:, 3, :], ACT.Sqrt).then_inc(root, 1)
                act.preload_act_table_set("natural_log_exp_and_others")
                t_high(n, 0, 0)

            next_image(0)
            t_high(0, 1, 1)
            act.wait_ge(bc_ready, 2)
            with act.Fori(0, N) as n:
                chunk_qkv(n, 0, 0, True, True)
                chunk_qkv(n, 1, 1, False, True)
                with act.Fori(1, NCK // 2 - 1) as pair:
                    for e in range(2):
                        chunk_qkv(n, pair * 2 + e, e, False, True)
                chunk_qkv(n, NCK - 2, 0, False, True)
                chunk_qkv(n, NCK - 1, 1, False, False)
                k_exp(n, 0, 1, True)
                k_exp(n, 1, 0, False)
                q_copy(n, NCK - 1, 1)
                k_exp(n, 1, 1, False)
                with act.Fori(2, NCK) as c:
                    for o in range(KT):
                        k_exp(n, c, o, False)
                next_image(n + 1)
                act.wait_ge(y_stored, 16 * (n * NCK + 1))
                for e in range(2):
                    square(n, e, e)
                    y_copy(n, e, e, True)
                inverse_deviation(n, 0, 0)
                with act.Fori(1, NCK // 2) as pair:
                    for e in range(2):
                        square(n, pair * 2 + e, e)
                        inverse_deviation(n, pair * 2 + e - 1, 1 - e)
                        y_copy(n, pair * 2 + e, e, False)
                        store(n, pair * 2 + e - 2)
                inverse_deviation(n, NCK - 1, 1)
                store(n, NCK - 2)
                t_high(n + 1, 1, 1)
                store(n, NCK - 1)

        @block.vector
        def _(dve):
            def heads(ap):
                return ap.rearrange("p t (a d) -> p t a d", d=DH)

            def t_norm(n, c, half, first=False):
                if not first:
                    dve.wait_ge(tl_ready, n * NCK + c)
                for k in range(KT):
                    ins = dve.tensor_scalar(tf[:, k, :], xb[:, half, k, chunk(c)], ab[:, 0, k:k + 1],
                                            ab[:, 1, k:k + 1], ALU.mult, ALU.add)
                ins.then_inc(t_normed, 1)

            def q_shift(n, c, h):
                i = n * NP + c * 2 + h
                dve.wait_ge(qv_mm, i + 1)
                src = heads(ps[:, 2 * h:2 * h + 2, 0:C])
                dve.tensor_reduce(rq[:, h, 0, :], src, AX.X, ALU.max).then_inc(q_maxed, 1)
                dve.wait_ge(q_maxed, i + 1)
                dve.tensor_tensor(heads(qs[:, h, :, :]), src,
                                  rq[:, h, 0, :].rearrange("p (t a) -> p t a", t=2).unsqueeze(3)
                                  .to_broadcast([P, 2, HEADS, DH]), ALU.subtract).then_inc(q_shifted, 1)

            def q_sum(n, c, h):
                i = n * NP + c * 2 + h
                dve.wait_ge(q_exped, i + 1)
                dve.tensor_reduce(rq[:, h, 1, :], heads(qs[:, h, :, :]), AX.X, ALU.add).then_inc(q_summed, 1)
                dve.wait_ge(q_summed, i + 1)
                dve.reciprocal(rq[:, h, 2, :], rq[:, h, 1, :]).then_inc(q_inv, 1)

            def k_copy(n, c, o):
                dve.wait_ge(k_mm, n * NS + c * KT + o + 1)
                dve.tensor_scalar(kraw[:, o, chunk(c)], ps[:, 4 + o, :], 1.0, None, ALU.mult, ALU.max,
                                  accum_out=kst[:, o, 0, bass.ds(c, 1)]).then_inc(k_copied, 1)

            def k_max(n, o):
                dve.wait_ge(k_copied, (n + 1) * NS - 1 + o)
                dve.tensor_reduce(kcol[:, 0, o:o + 1], kst[:, o, 0, :], AX.X, ALU.max,
                                  negate=True).then_inc(k_negmax, 1)

            def kT_copy(n, c, o, first):
                if not first:
                    dve.wait_ge(ctx_mm, n * NS + c * KT + o - 1)
                dve.wait_ge(k_turned, n * NS + c * KT + o + 1)
                dve.tensor_copy(kT[:, o, :], ps[:, 4 + o, :]).then_inc(kT_ready, 1)

            def z_and_y(n, c, par, half):
                dve.wait_ge(rstd_ready, n * NCK + c + 1)
                for o in range(KT):
                    ins = tt(yb[:, par, o, :], yb[:, par, o, :], rstd[:, par, :], ALU.mult)
                ins.then_inc(z_ready, 1)
                dve.wait_ge(z_ready, n * NCK + c + 1)
                for o in range(KT):
                    at = xb[:, half, o, chunk(c)]
                    ins = dve.scalar_tensor_tensor(out=at, in0=yb[:, par, o, :], scalar=pr[:, C_LNG + o:C_LNG + o + 1],
                                                   in1=at, op0=ALU.mult, op1=ALU.add)
                ins.then_inc(y_ready, 1)

            tt = dve.tensor_tensor
            mean, var = mv[:, :, 0], mv[:, :, 1]

            class Steps:

                def __init__(self, sem, first, done=0):
                    self.sem, self.first, self.done = sem, first, done

                def __call__(self, ins):
                    self.done += 1
                    ins.then_inc(self.sem, 1)
                    dve.wait_ge(self.sem, self.first + self.done)

            def channel_means(n):
                link = Steps(step, n * G_STEPS)
                dve.wait_ge(stats, (n + 1) * NCK)
                dve.memset(tick[:, 0:1], 0.0)
                for k in range(KT):
                    ins = dve.bn_aggr(mv[:, k, :], bst[:, k, :, :])
                link(ins)
                dve.tensor_copy(me[:, 0, :], mean)
                link(tt(sm[:, 0, :], mean, mean, ALU.mult))
                link(tt(me[:, 1, :], sm[:, 0, :], var, ALU.add))

            def norm_columns(n):
                link = Steps(step, n * G_STEPS, 3)
                dve.wait_ge(gp_done, n + 1)
                link(dve.tensor_copy(gs[:].rearrange("p a k -> p (a k)"), ps[:, 6, 0:2 * KT]))
                link(tt(sm[:, 1, :], gs[:, 0, :], gs[:, 0, :], ALU.mult))
                link(tt(sm[:, 2, :], gs[:, 1, :], sm[:, 1, :], ALU.subtract))
                link(dve.tensor_scalar(sm[:, 3, :], sm[:, 2, :], EPS_GN, None, ALU.add))
                assert link.done == G_ROOT
                dve.wait_ge(root, n + 1)
                link(dve.reciprocal(ab[:, 0, :], sm[:, 4, :]))
                link(dve.scalar_tensor_tensor(out=ab[:, 1, :], in0=gs[:, 0, :], scalar=-1.0, in1=ab[:, 0, :],
                                              op0=ALU.mult, op1=ALU.mult))
                assert link.done == G_STEPS

            def chunk_stats(c, buf):
                for k in range(KT):
                    ins = dve.bn_stats(bst[:, k, bass.ds(c, 1), :].rearrange("p a s -> p (a s)"),
                                       xb[:, buf, k, chunk(c)])
                ins.then_inc(stats, 1)

            for c in range(NCK):
                if c % (NCK // PIECES) == 0:
                    dve.wait_ge(x_piece[c // (NCK // PIECES)], 16)
                chunk_stats(c, 0)
            channel_means(0)
            norm_columns(0)
            t_norm(0, 0, 0, True)
            dve.wait_ge(w_loaded, 48)
            dve.wait_ge(consts, 5)
            dve.wait_ge(b_mean, 1)
            dve.tensor_copy(bsum[:], ps[:, 0, 0:1]).then_inc(bc_ready, 1)
            dve.wait_ge(bc_ready, 1)
            dve.tensor_scalar(bc[:], pr[:, C_BOUT:C_BOUT + KT], bsum[:], None,
                              ALU.subtract).then_inc(bc_ready, 1)
            for k in range(KT):
                dve.wait_ge(wh_ready, k + 1)
                for dst, src in ((0, 0), (C, 2 * C), (2 * C, C)):
                    ins = dve.tensor_tensor(wl[:, k, dst:dst + C], wf[:, k, src:src + C],
                                            wh[:, k, dst:dst + C].bitcast(F32), ALU.subtract)
                ins.then_inc(wl_ready, 1)
            dve.tensor_reduce(wsum[:, 0, :], wo[:], AX.X, ALU.add).then_inc(wo_step, 1)
            dve.wait_ge(wo_step, 1)
            dve.tensor_scalar(wsum[:, 1, :], wsum[:, 0, :], -1.0 / C, None, ALU.mult).then_inc(wo_step, 1)
            dve.wait_ge(wo_step, 2)
            for k in range(KT):
                ins = dve.tensor_scalar(wo[:, k, :], wo[:, k, :], wsum[:, 1, k:k + 1], None, ALU.add)
            ins.then_inc(wo_step, 1)
            t_norm(0, 1, 0)
            with dve.Fori(0, N // 2) as two:
              for half in range(2):
                n = two * 2 + half

                def chunk_qk(c, last=False):
                    for h in range(2):
                        q_shift(n, c, h)
                        k_copy(n, c, h)
                        if last:
                            k_max(n, h)
                        q_sum(n, c, h)

                chunk_qk(0)
                with dve.Fori(1, NCK - 1) as c:
                    t_norm(n, c + 1, half)
                    chunk_qk(c)
                chunk_qk(NCK - 1, True)
                dve.wait_ge(x_loaded[1 - half], two * 16 * KT + 16 * KT)
                for o in range(KT):
                    kT_copy(n, 0, o, True)
                chunk_stats(0, 1 - half)
                with dve.Fori(1, NCK) as c:
                    for o in range(KT):
                        kT_copy(n, c, o, False)
                    chunk_stats(c, 1 - half)
                mlink = Steps(m_step, n * M_STEPS)
                dve.wait_ge(k_exped, (n + 1) * NS)
                mlink(dve.tensor_reduce(kcol[:, 1, :], kst[:, :, 1, :], AX.X, ALU.add))
                mlink(dve.reciprocal(kcol[:, 2, :], kcol[:, 1, :]))
                dve.wait_ge(ctx_mm, (n + 1) * NS)
                for g in range(KT):
                    for a in range(P // DH):
                        r = slice(a * DH, (a + 1) * DH)
                        ins = dve.tensor_scalar(cm[r, g, r], ps[r, 6 + g, r], DH ** -0.5 / L, None, ALU.mult)
                mlink(ins)
                dve.wait_ge(m_mm, 2 * n + 1)
                mlink(dve.tensor_copy(kraw[:, 0, 4 * C:5 * C], ps[:, 0, 0:KT * P]))
                channel_means(n + 1)
                dve.wait_ge(m_mm, 2 * n + 2)
                for g in range(KT):
                    ins = dve.tensor_scalar(mT[:, g, :], ps[:, 1, g * C:(g + 1) * C], kcol[:, 2, g:g + 1], None,
                                            ALU.mult)
                ins.then_inc(m_step, 1)
                norm_columns(n + 1)
                t_norm(n + 1, 0, 1 - half, True)
                with dve.Fori(0, NCK // 2 - 1) as pair:
                    for e in range(2):
                        z_and_y(n, pair * 2 + e, e, half)
                z_and_y(n, NCK - 2, 0, half)
                t_norm(n + 1, 1, 1 - half)
                z_and_y(n, NCK - 1, 1, half)


G_ROOT, G_STEPS, M_STEPS = 7, 9, 5


def program(nc, x, par, wth, wph, wg, wout, wqkv, wo, y):
    x1 = nc.dram_tensor("x1_between", [N, C, L], F32, kind="Internal").ap()
    nonlocal_block(nc, x, par, wth, wph, wg, wout, x1)
    linear_attention_block(nc, x1, par, wqkv, wo, y)


def kernel(**inputs):
    import numpy as np
    import concourse.bacc as bacc
    from concourse.bass_utils import run_bass_kernel_spmd

    def columns(a):
        return np.asarray(a).reshape(-1, P).T

    i = {name: np.asarray(a) for name, a in inputs.items()}
    par = np.concatenate([columns(a) for a in (
        i["L0_conv_cfc"][:, 0], i["L0_conv_cfc"][:, 1], i["L0_conv_theta_b"], i["L0_conv_phi_b"], i["L0_conv_g_b"],
        i["L0_conv_out_b"], i["L1_conv_b_out"], i["L1_conv_g"])], axis=1)
    arrays = {"x": i["x"].reshape(N, C, L), "par": par, "wth": i["L0_conv_theta_w"].T, "wph": i["L0_conv_phi_w"].T,
              "wg": i["L0_conv_g_w"].T, "wout": i["L0_conv_out_w"].T, "wqkv": i["L1_conv_w_qkv"].T,
              "wo": i["L1_conv_w_out"].T}
    nc = bacc.Bacc("TRN2", target_bir_lowering=False, num_devices=1)
    fed, args = {}, []
    for name, a in arrays.items():
        fed[f"in_{name}"] = np.ascontiguousarray(a)
        args.append(nc.dram_tensor(f"in_{name}", a.shape, mybir.dt.from_np(a.dtype), kind="ExternalInput").ap())
    args.append(nc.dram_tensor("out_y", [N, C, L], F32, kind="ExternalOutput").ap())
    program(nc, *args)
    r = run_bass_kernel_spmd(nc, [fed], core_ids=[0])
    return r.results[0]["out_y"].reshape(N, C, 64, 64)
```
